# Optimizing a Trainium2 kernel written in Bass

```python
import numpy as np
import jax
import jax.numpy as jnp

def _softmax(x, axis=-1):
    return jax.nn.softmax(x, axis=axis)

def _gelu(x):
    return jax.nn.gelu(x, approximate=True)

def _silu(x):
    return jax.nn.silu(x)

def _sigmoid(x):
    return jax.nn.sigmoid(x)

def _layernorm(x, axis=-1, eps=1e-05):
    m = jnp.mean(x, axis=axis, keepdims=True)
    v = jnp.var(x, axis=axis, keepdims=True)
    return (x - m) / jnp.sqrt(v + eps)

def _scatter_add(tgt, idx, src, axis=0):
    return tgt.at[idx].add(src)

def _segment_sum(src, seg, n):
    return jax.ops.segment_sum(src, seg, n)
kernel_name = 'mk_sandwich_d1_jaxref_r8_3201db'

def setup_inputs(seed: int=0):
    np.random.seed(seed)
    _w = jnp.asarray

    def _L0_attn_setup():
        import jax, jax.numpy as jnp
        import numpy as np
        NUM_HEADS = 16
        EMBED_DIM = 128

        def _linear_attention(x, Wq, bq, Wk, bk, Wv, bv, Wo, bo):
            B, S, D = x.shape
            H = NUM_HEADS
            hd = D // H
            v = (x @ Wv + bv).reshape(B, S, H, hd)
            q = (x @ Wq + bq).reshape(B, S, H, hd)
            k = (x @ Wk + bk).reshape(B, S, H, hd)
            q = jax.nn.elu(q) + 1.0
            k = jax.nn.elu(k) + 1.0
            qT = q.transpose(1, 0, 2, 3)
            kT = k.transpose(1, 0, 2, 3)
            vT = v.transpose(1, 0, 2, 3)
            s0 = jnp.zeros((B, H, hd, hd), dtype=x.dtype)
            z0 = jnp.zeros((B, H, hd), dtype=x.dtype)

            def step(carry, qkv):
                s, z = carry
                q_i, k_i, v_i = qkv
                s = s + jnp.einsum('bhd,bhm->bhdm', k_i, v_i)
                z = z + k_i
                qs = jnp.einsum('bhd,bhdm->bhm', q_i, s)
                qz = jnp.einsum('bhd,bhd->bh', q_i, z)[..., None]
                return ((s, z), qs / (qz + 1e-06))
            (_, _), values = jax.lax.scan(step, (s0, z0), (qT, kT, vT))
            values = values.transpose(1, 0, 2, 3).reshape(B, S, D)
            return values @ Wo + bo
        key = jax.random.key(seed)
        ks = jax.random.split(key, 6)
        B, S, D = (4, 256, EMBED_DIM)
        sc = 1.0 / np.sqrt(D)
        return {'x': jax.random.normal(ks[0], (B, S, D), dtype=jnp.float32), 'mask': jnp.ones((B, S), dtype=jnp.int32), 'Wq': jax.random.normal(ks[1], (D, D), dtype=jnp.float32) * sc, 'bq': jnp.zeros((D,), dtype=jnp.float32), 'Wk': jax.random.normal(ks[2], (D, D), dtype=jnp.float32) * sc, 'bk': jnp.zeros((D,), dtype=jnp.float32), 'Wv': jax.random.normal(ks[3], (D, D), dtype=jnp.float32) * sc, 'bv': jnp.zeros((D,), dtype=jnp.float32), 'Wo': jax.random.normal(ks[4], (D, D), dtype=jnp.float32) * sc, 'bo': jnp.zeros((D,), dtype=jnp.float32)}
    _L0_attn_in = _L0_attn_setup()

    def _L0_ffn_setup():
        import jax, jax.numpy as jnp
        import numpy as np
        E = 16
        H = 128
        F = 256
        TOP_K = 1
        B, S = (2, 128)
        key = jax.random.key(seed)
        ks = jax.random.split(key, 7)
        s = 0.02
        return {'hidden_states': jax.random.normal(ks[0], (B, S, H), jnp.float32), 'w_router': jax.random.normal(ks[1], (E, H), jnp.float32) * s, 'gate_up_proj': jax.random.normal(ks[2], (E, H, 2 * F), jnp.float32) * s, 'down_proj': jax.random.normal(ks[3], (E, F, H), jnp.float32) * s, 'w_gate': jax.random.normal(ks[4], (F, H), jnp.float32) * s, 'w_up': jax.random.normal(ks[5], (F, H), jnp.float32) * s, 'w_down': jax.random.normal(ks[6], (H, F), jnp.float32) * s}
    _L0_ffn_in = _L0_ffn_setup()
    _d = {'L0_attn_x': _L0_attn_in['x'], 'L0_attn_mask': _L0_attn_in['mask'], 'L0_attn_Wq': _L0_attn_in['Wq'], 'L0_attn_bq': _L0_attn_in['bq'], 'L0_attn_Wk': _L0_attn_in['Wk'], 'L0_attn_bk': _L0_attn_in['bk'], 'L0_attn_Wv': _L0_attn_in['Wv'], 'L0_attn_bv': _L0_attn_in['bv'], 'L0_attn_Wo': _L0_attn_in['Wo'], 'L0_attn_bo': _L0_attn_in['bo'], 'L0_ffn_w_router': _L0_ffn_in['w_router'], 'L0_ffn_gate_up_proj': _L0_ffn_in['gate_up_proj'], 'L0_ffn_down_proj': _L0_ffn_in['down_proj'], 'L0_ffn_w_gate': _L0_ffn_in['w_gate'], 'L0_ffn_w_up': _L0_ffn_in['w_up'], 'L0_ffn_w_down': _L0_ffn_in['w_down']}
    _x0 = _d['L0_attn_x']
    _d['L0_attn_x'] = jax.random.normal(jax.random.fold_in(jax.random.key(seed), 1), (16, 256, 128), dtype=_x0.dtype)
    del _x0
    return _d

def reference(L0_attn_x, L0_attn_mask, L0_attn_Wq, L0_attn_bq, L0_attn_Wk, L0_attn_bk, L0_attn_Wv, L0_attn_bv, L0_attn_Wo, L0_attn_bo, L0_ffn_w_router, L0_ffn_gate_up_proj, L0_ffn_down_proj, L0_ffn_w_gate, L0_ffn_w_up, L0_ffn_w_down):

    def _L0_attn_ref(x, mask, Wq, bq, Wk, bk, Wv, bv, Wo, bo):
        import jax, jax.numpy as jnp
        import numpy as np
        NUM_HEADS = 16
        EMBED_DIM = 128

        def _linear_attention(x, Wq, bq, Wk, bk, Wv, bv, Wo, bo):
            B, S, D = x.shape
            H = NUM_HEADS
            hd = D // H
            v = (x @ Wv + bv).reshape(B, S, H, hd)
            q = (x @ Wq + bq).reshape(B, S, H, hd)
            k = (x @ Wk + bk).reshape(B, S, H, hd)
            q = jax.nn.elu(q) + 1.0
            k = jax.nn.elu(k) + 1.0
            qT = q.transpose(1, 0, 2, 3)
            kT = k.transpose(1, 0, 2, 3)
            vT = v.transpose(1, 0, 2, 3)
            s0 = jnp.zeros((B, H, hd, hd), dtype=x.dtype)
            z0 = jnp.zeros((B, H, hd), dtype=x.dtype)

            def step(carry, qkv):
                s, z = carry
                q_i, k_i, v_i = qkv
                s = s + jnp.einsum('bhd,bhm->bhdm', k_i, v_i)
                z = z + k_i
                qs = jnp.einsum('bhd,bhdm->bhm', q_i, s)
                qz = jnp.einsum('bhd,bhd->bh', q_i, z)[..., None]
                return ((s, z), qs / (qz + 1e-06))
            (_, _), values = jax.lax.scan(step, (s0, z0), (qT, kT, vT))
            values = values.transpose(1, 0, 2, 3).reshape(B, S, D)
            return values @ Wo + bo
        return _linear_attention(x, Wq, bq, Wk, bk, Wv, bv, Wo, bo)

    def _L0_ffn_ref(hidden_states, w_router, gate_up_proj, down_proj, w_gate, w_up, w_down):
        import jax, jax.numpy as jnp
        import numpy as np
        E = 16
        H = 128
        F = 256
        TOP_K = 1
        B, S = (2, 128)
        b, s, h = hidden_states.shape
        x = hidden_states.reshape(-1, h)
        logits = x @ w_router.T
        _, top_idx = jax.lax.top_k(logits, TOP_K)
        mask = jax.nn.one_hot(top_idx, E, dtype=logits.dtype).sum(axis=1)
        scores = jax.nn.sigmoid(logits) * mask
        masked_inputs = scores.T[:, :, None] * x[None, :, :]
        gate_up = jnp.einsum('eth,ehf->etf', masked_inputs, gate_up_proj)
        gate, up = jnp.split(gate_up, 2, axis=-1)
        expert_out = jnp.einsum('etf,efh->eth', up * jax.nn.silu(gate), down_proj)
        shared = jax.nn.silu(x @ w_gate.T) * (x @ w_up.T) @ w_down.T
        out = shared + expert_out.sum(axis=0)
        return out.reshape(b, s, h)
    x = L0_attn_x
    x = x + _layernorm(_L0_attn_ref(_layernorm(x, axis=-1), L0_attn_mask, L0_attn_Wq, L0_attn_bq, L0_attn_Wk, L0_attn_bk, L0_attn_Wv, L0_attn_bv, L0_attn_Wo, L0_attn_bo), axis=-1)
    x = x + _layernorm(_L0_ffn_ref(_layernorm(x, axis=-1), L0_ffn_w_router, L0_ffn_gate_up_proj, L0_ffn_down_proj, L0_ffn_w_gate, L0_ffn_w_up, L0_ffn_w_down), axis=-1)
    return x

_drawn_inputs = setup_inputs


def setup_inputs(seed=0):
    import zlib

    import numpy as np

    out = dict(_drawn_inputs(seed))
    spreads = {'L0_attn_bq': (0.0, 0.4),
     'L0_attn_bk': (0.0, 0.464),
     'L0_attn_bv': (0.0, 0.1),
     'L0_attn_bo': (0.0, 0.1)}
    factors = {}
    for name, (base, spread) in spreads.items():
        noise = np.random.default_rng([zlib.crc32(name.encode()), seed]).standard_normal(out[name].shape)
        drawn = base * np.exp(spread * noise) if base else spread * noise
        out[name] = jnp.asarray(drawn.astype(out[name].dtype))
    for name, factor in factors.items():
        out[name] = (out[name] * factor).astype(out[name].dtype)
    return out
```

```python
from contextlib import ExitStack

import concourse.bass as bass
from concourse import mybir

F32 = mybir.dt.float32
BF16 = mybir.dt.bfloat16
I32 = mybir.dt.int32
U32 = mybir.dt.uint32
ALU = mybir.AluOpType
ACT = mybir.ActivationFunctionType
AX = mybir.AxisListType.X

P = 128
EPS = 1e-5
EPS_DEN = 1e-6
RSQRT_MAGIC = float(0x5F3759DF)


def live(index, count):
    return not isinstance(index, int) or 0 <= index < count


def at_least(eng, sem, count):
    if not isinstance(count, int) or count > 0:
        eng.wait_ge(sem, count)


def run_steps(eng, body, first, lo, hi, last, unroll):
    assert (hi - lo) % unroll == 0
    for s in range(first, lo):
        body(s, s % unroll)
    with eng.Fori(0, (hi - lo) // unroll) as i:
        for u in range(lo, lo + unroll):
            body(i * unroll + u, u % unroll)
    for s in range(hi, last):
        body(s, s % unroll)


def build(nc, x, wq, wk, wv, wo, bq, bk, bv, bo, w_router_t, gate_up, down, w_gate_t, w_up_t, w_down_t, out):
    B, S, D = x.shape
    NH = 16
    HD = D // NH
    E = w_router_t.shape[1]
    F = w_gate_t.shape[1]
    FC = F // P
    NT = B * S // P
    TPB = S // P
    SLOT_TILES = (B * S + E * (P - 1)) // P
    NG = NT // 4
    KVW = NH * HD * HD
    assert D == P and TPB == 2 and NT % 4 == 0

    x_dram = x.rearrange("b s d -> (b s) d").rearrange("(t p) d -> p t d", p=P)
    out_dram = out.rearrange("b s d -> (b s) d").rearrange("(t p) d -> p t d", p=P)
    sorted_x = nc.dram_tensor("sorted_x", (SLOT_TILES * P, D), F32, kind="Internal").ap()
    sorted_y = nc.dram_tensor("sorted_y", (SLOT_TILES * P, D), F32, kind="Internal").ap()
    sorted_x_tiles = sorted_x.rearrange("(j p) d -> p j d", p=P)
    sorted_y_tiles = sorted_y.rearrange("(j p) d -> p j d", p=P)

    with ExitStack() as ctx:
        def sb(name, shape, dt=F32):
            return ctx.enter_context(nc.sbuf_tensor(name, shape, dt))

        def sem(name):
            return ctx.enter_context(nc.semaphore(name))

        col_index = sb("col_index", [P, P])
        row_index = sb("row_index", [P, 1])
        ident = sb("ident", [P, P])
        upto = sb("upto", [P, P])
        ones = sb("ones", [P, P])
        before_bf = sb("before_bf", [P, P], BF16)
        ones_bf = sb("ones_bf", [P, P], BF16)
        slot_start = sb("slot_start", [1, SLOT_TILES])
        wait_taker = sb("wait_taker", [P, 1])
        zeros = sb("zeros", [P, D])
        w_qkv = sb("w_qkv", [P, 3 * D])
        w_o = sb("w_o", [P, D])
        w_r = sb("w_r", [P, E])
        w_g = sb("w_g", [P, F])
        w_u = sb("w_u", [P, F])
        w_d = sb("w_d", [P, FC, D])
        w_exp = sb("w_exp", [P, E, 2 * F])
        w_exp_down = sb("w_exp_down", [P, E, FC, D])
        bias = sb("bias", [P, 4 * D])
        bias_left = sb("bias_left", [P, 4 * D])
        bias_part = sb("bias_part", [P, 3, 4 * D], BF16)
        bias_rows = sb("bias_rows", [P, 4 * D], BF16)
        x_all = sb("x_all", [P, NT, D])
        y_all = sb("y_all", [P, NT, D])
        rs1 = sb("rs1", [P, NT])
        nm1 = sb("nm1", [P, NT])
        rs2 = sb("rs2", [P, NT])
        nm2 = sb("nm2", [P, NT])
        stats = sb("stats", [P, NT, 6])
        top = sb("top", [P, NT])
        first_top = sb("first_top", [P, NT])
        from_last = sb("from_last", [P, E])
        is_top = sb("is_top", [P, 4, E])
        newton = sb("newton", [P, 4, NT // 4])
        newton2 = sb("newton2", [P, 4, 2, 4])
        xn = sb("xn", [P, 2, D])
        xnT = sb("xnT", [P, 2, D])
        ex = sb("ex", [P, 2, 2 * D])
        rl = sb("rl", [P, 2, 2 * D])
        qk = sb("qk", [P, 4, 2 * D])
        vv = sb("vv", [P, 2, D])
        kv = sb("kv", [P, 4, KVW])
        zq = sb("zq", [P, D])
        den = sb("den", [P, NH])
        rden = sb("rden", [P, NH])
        prod = sb("prod", [P, KVW])
        num = sb("num", [P, D])
        att = sb("att", [P, 2, D])
        attT = sb("attT", [P, D])

        ps = [ctx.enter_context(nc.psum_tensor(f"bank{i}", [P, 512], F32)) for i in range(8)]

        s_x = [sem(f"x_loaded{i}") for i in range(4)]
        s_w = sem("attention_weights_loaded")
        s_bias = sem("bias_loaded")
        s_w2 = sem("ffn_weights_loaded")
        s_wexp = sem("expert_weights_loaded")
        s_iota = sem("indices_written")
        s_const = sem("constants_written")
        s_zero = sem("zeros_written")
        s_cleared = sem("sorted_x_cleared")
        s_setup = sem("setup_steps")
        s_norm1 = sem("norm1_ready")
        s_xn = sem("xn_ready")
        s_xn_t = sem("xn_transposed")
        s_xnT = sem("xnT_ready")
        s_qkv = sem("qkv_projected")
        s_elu = sem("elu_halves_ready")
        s_v = sem("v_ready")
        s_qk = sem("qk_ready")
        s_kv = sem("kv_ready")
        s_z = sem("z_summed")
        s_s = sem("state_summed")
        s_chain = sem("attention_steps")
        s_att = sem("att_ready")
        s_att_t = sem("att_transposed")
        s_attT = sem("attT_ready")
        s_y = sem("y_projected")
        s_y_out = sem("y_stored")

        def linker(eng, chain_sem, base):
            count = [0]

            def link(ins, before_bn_stats=False):
                count[0] += 1
                ins.then_inc(chain_sem, 1)
                eng.wait_ge(chain_sem, base + count[0])
                if before_bn_stats:
                    nc.vector.memset(wait_taker[:], 0.0)
            return link

        def rstd_of(link, st, scratch, rs, nm):
            mean_even, sq_even, mean_odd, sq_odd = st[1], st[2], st[4], st[5]
            ve, y, t, mean2 = (scratch[:, n] for n in range(4))
            tensor, scalar = nc.vector.tensor_tensor, nc.vector.tensor_scalar
            fused = nc.vector.scalar_tensor_tensor
            tensor(mean2, mean_even, mean_odd, ALU.add)
            tensor(t, mean_even, mean_odd, ALU.subtract)
            link(tensor(ve, sq_even, sq_odd, ALU.add))
            link(fused(out=t, in0=t, scalar=0.25, in1=t, op0=ALU.mult, op1=ALU.mult))
            link(fused(out=ve, in0=ve, scalar=1.0 / D, in1=t, op0=ALU.mult, op1=ALU.add))
            link(scalar(ve, ve, EPS, None, ALU.add))
            link(scalar(t.bitcast(I32), ve.bitcast(I32), 1, None, ALU.logical_shift_right))
            link(scalar(y.bitcast(I32), t.bitcast(I32), -1.0, RSQRT_MAGIC, ALU.mult, ALU.add))
            for k in range(3):
                link(tensor(t, y, y, ALU.mult))
                link(fused(out=t, in0=t, scalar=-0.5, in1=ve, op0=ALU.mult, op1=ALU.mult))
                link(fused(out=rs if k == 2 else y, in0=t, scalar=1.5, in1=y, op0=ALU.add, op1=ALU.mult))
            return fused(out=nm, in0=mean2, scalar=-0.5, in1=rs, op0=ALU.mult, op1=ALU.mult)

        ps_qkv = [ps[0], ps[1]]
        ps_s = [(ps[2], ps[3]), (ps[4], ps[5])]
        ps_xT, ps_o = ps[6], ps[7]
        XC = NT // 4
        CH = 6

        with nc.Block() as block:
            @block.sync
            def _(sp):
                for c in range(4):
                    sp.dma_start(x_all[:, c * XC:(c + 1) * XC, :],
                                 x_dram[:, c * XC:(c + 1) * XC, :]).then_inc(s_x[c], 16)
                    if c == 0:
                        for n, w in enumerate((wq, wk, wv)):
                            sp.dma_start(w_qkv[:, n * D:(n + 1) * D], w).then_inc(s_w, 16)
                        sp.dma_start(w_o[:], wo).then_inc(s_w, 16)
                sp.dma_start(w_r[:], w_router_t).then_inc(s_w2, 16)
                sp.dma_start(w_g[:], w_gate_t).then_inc(s_w2, 16)
                sp.dma_start(w_u[:], w_up_t).then_inc(s_w2, 16)
                sp.dma_start(w_d[:], w_down_t.rearrange("(c f) h -> f c h", f=P)).then_inc(s_w2, 16)
                for e in range(0, E, 4):
                    sp.dma_start(w_exp[:, e:e + 4, :],
                                 gate_up[e:e + 4].rearrange("e h f -> h e f")).then_inc(s_wexp, 16)
                    for c in range(FC):
                        sp.dma_start(w_exp_down[:, e:e + 4, c, :],
                                     down[e:e + 4, c * P:(c + 1) * P].rearrange("e f h -> f e h")).then_inc(s_wexp, 16)
                sp.wait_ge(s_zero, 1)
                for j in range(SLOT_TILES):
                    sp.dma_start(sorted_x_tiles[:, j, :], zeros[:]).then_inc(s_cleared, 16)

            @block.gpsimd
            def _(pool):
                for n, b in enumerate((bq, bk, bv, bo)):
                    pool.dma_start(bias[:, n * D:(n + 1) * D],
                                   b.rearrange("(o d) -> o d", o=1).to_broadcast([P, D])).then_inc(s_bias, 16)
                nc.gpsimd.iota(col_index[:], [[1, P]], 0, 0, allow_small_or_imprecise_dtypes=True).then_inc(s_iota, 1)
                nc.gpsimd.iota(row_index[:], [[0, 1]], 0, 1, allow_small_or_imprecise_dtypes=True).then_inc(s_iota, 1)
                nc.gpsimd.iota(slot_start[:], [[P, SLOT_TILES]], 0, 0,
                               allow_small_or_imprecise_dtypes=True).then_inc(s_iota, 1)
                nc.gpsimd.memset(zeros[:], 0.0).then_inc(s_zero, 1)

                def step(t, u):
                    pool.wait_ge(s_qk, t + 1)
                    pool.wait_ge(s_v, t + 1)
                    at_least(pool, s_s, t - 2)
                    k = qk[:, u, D:2 * D].rearrange("p (h o d) -> p h o d", h=NH, o=1).to_broadcast([P, NH, HD, HD])
                    v = vv[:, u % 2, :].rearrange("p (h m o) -> p h m o", h=NH, o=1).to_broadcast([P, NH, HD, HD])
                    nc.gpsimd.tensor_tensor(kv[:, u, :].rearrange("p (h m d) -> p h m d", h=NH, m=HD),
                                            k, v, ALU.mult).then_inc(s_kv, 1)
                run_steps(pool, step, 0, 4, NT, NT, 4)

            @block.scalar
            def _(act):
                def step(t, u):
                    if live(t + 4, NT):
                        if isinstance(t, int) and (t + 4) % XC == 0:
                            act.wait_ge(s_norm1, (t + 4) // XC + 1)
                        elif not isinstance(t, int):
                            act.wait_ge(s_norm1, 4)
                        at_least(act, s_xn_t, t + 3)
                        n = (t + 4) if isinstance(t, int) else bass.ds(t + 4, 1)
                        i = slice(t + 4, t + 5) if isinstance(t, int) else n
                        nc.scalar.activation(xn[:, u % 2, :], x_all[:, i, :].rearrange("p o d -> p (o d)"),
                                             ACT.Identity, bias=nm1[:, i], scale=rs1[:, i]).then_inc(s_xn, 1)
                    if live(t + 3, NT):
                        act.wait_ge(s_xn_t, t + 4)
                        at_least(act, s_qkv, t + 2)
                        nc.scalar.copy(xnT[:, (u + 3) % 2, :], ps_xT[:, 0:D]).then_inc(s_xnT, 1)
                    if live(t - 1, NT):
                        act.wait_ge(s_att_t, t)
                        at_least(act, s_y, t - 1)
                        nc.scalar.copy(attT[:], ps_o[:, 0:D]).then_inc(s_attT, 1)
                    if live(t + 2, NT):
                        act.wait_ge(s_qkv, t + 3)
                        at_least(act, s_qk, t + 1)
                        nc.scalar.activation(ex[:, u % 2, :], ps_qkv[u % 2][:, 0:2 * D], ACT.Exp).then_inc(s_elu, 1)
                        nc.scalar.activation(rl[:, u % 2, :], ps_qkv[u % 2][:, 0:2 * D], ACT.Relu).then_inc(s_elu, 1)
                        at_least(act, s_kv, t + 1)
                        nc.scalar.copy(vv[:, u % 2, :], ps_qkv[u % 2][:, 2 * D:3 * D]).then_inc(s_v, 1)
                    if live(t - 1, NT):
                        act.wait_ge(s_y, t)
                        i = slice(t - 1, t) if isinstance(t, int) else bass.ds(t - 1, 1)
                        nc.scalar.copy(y_all[:, i, :].rearrange("p o d -> p (o d)"), ps_o[:, D:2 * D]).then_inc(s_y_out, 1)
                run_steps(act, step, -4, 4, 28, NT + 1, 4)

            @block.vector
            def _(dve):
                link = linker(dve, s_setup, 0)
                dve.wait_ge(s_iota, 2)
                nc.vector.tensor_scalar(ident[:], col_index[:], row_index[:], None, ALU.is_equal).then_inc(s_const, 1)
                nc.vector.tensor_scalar(upto[:], col_index[:], row_index[:], None, ALU.is_ge).then_inc(s_const, 1)
                nc.vector.memset(ones[:], 1.0).then_inc(s_const, 1)
                nc.vector.memset(ones_bf[:], 1.0).then_inc(s_const, 1)
                nc.vector.tensor_scalar(before_bf[:], col_index[:], row_index[:], None, ALU.is_gt).then_inc(s_const, 1)
                nc.vector.tensor_scalar(from_last[:], col_index[:, 0:E], -1.0, float(E), ALU.mult, ALU.add).then_inc(s_const, 1)
                link(nc.vector.memset(bias_rows[:], 0.0))
                dve.wait_ge(s_bias, 64)
                link(nc.vector.tensor_copy(bias_part[:, 0, :], bias[:]))
                link(nc.vector.tensor_tensor(bias_left[:], bias[:], bias_part[:, 0, :], ALU.subtract))
                link(nc.vector.tensor_copy(bias_part[:, 1, :], bias_left[:]))
                link(nc.vector.tensor_tensor(bias_left[:], bias_left[:], bias_part[:, 1, :], ALU.subtract))
                link(nc.vector.tensor_copy(bias_part[:, 2, :], bias_left[:]))
                for n in range(3):
                    nc.vector.tensor_copy(bias_rows[32 * n:32 * n + 1, :],
                                          bias_part[32 * n:32 * n + 1, n, :]).then_inc(s_const, 1)
                for c in range(4):
                    dve.wait_ge(s_x[c], 16)
                    for t in range(c * XC, (c + 1) * XC):
                        ins = nc.vector.bn_stats(stats[:, t, :], x_all[:, t, :])
                    link(ins)
                    r = slice(c * XC, (c + 1) * XC)
                    rstd_of(link, [stats[:, r, n] for n in range(6)], newton, rs1[:, r], nm1[:, r]).then_inc(s_norm1, 1)

                def step(t, u):
                    if live(t, NT):
                        dve.wait_ge(s_z, t + 1)
                        at_least(dve, s_chain, CH * t)
                        q = qk[:, u, 0:D]
                        nc.vector.tensor_tensor(zq[:], ps_qkv[u % 2][:, 3 * D:4 * D], q, ALU.mult).then_inc(s_chain, 1)
                    if live(t + 1, NT):
                        dve.wait_ge(s_elu, 2 * (t + 2))
                        n = (u + 1) % 4
                        nc.vector.scalar_tensor_tensor(out=qk[:, n, :], in0=ex[:, n % 2, :], scalar=1.0,
                                                       in1=rl[:, n % 2, :], op0=ALU.min, op1=ALU.add).then_inc(s_qk, 1)
                    if live(t, NT):
                        dve.wait_ge(s_chain, CH * t + 1)
                        nc.vector.tensor_reduce(den[:], zq[:].rearrange("p (h d) -> p h d", h=NH), AX,
                                                ALU.add).then_inc(s_chain, 1)
                        dve.wait_ge(s_s, t + 1)
                        for half in range(2):
                            w = KVW // 2
                            qb = qk[:, u, half * D // 2:(half + 1) * D // 2].rearrange(
                                "p (h o d) -> p h o d", h=NH // 2, o=1).to_broadcast([P, NH // 2, HD, HD])
                            ins = nc.vector.tensor_tensor(
                                prod[:, half * w:(half + 1) * w].rearrange("p (h m d) -> p h m d", h=NH // 2, m=HD),
                                ps_s[u % 2][half][:].rearrange("p (h m d) -> p h m d", h=NH // 2, m=HD), qb, ALU.mult)
                        ins.then_inc(s_chain, 1)
                        dve.wait_ge(s_chain, CH * t + 2)
                        nc.vector.tensor_scalar(rden[:], den[:], EPS_DEN, None, ALU.add).then_inc(s_chain, 1)
                        dve.wait_ge(s_chain, CH * t + 3)
                        nc.vector.tensor_reduce(num[:], prod[:].rearrange("p (n d) -> p n d", d=HD), AX,
                                                ALU.add).then_inc(s_chain, 1)
                        dve.wait_ge(s_chain, CH * t + 4)
                        nc.vector.reciprocal(rden[:], rden[:]).then_inc(s_chain, 1)
                        dve.wait_ge(s_chain, CH * t + 6)
                        at_least(dve, s_att_t, t - 1)
                        nc.vector.tensor_tensor(att[:, u % 2, :].rearrange("p (h m) -> p h m", h=NH),
                                                num[:].rearrange("p (h m) -> p h m", h=NH),
                                                rden[:].rearrange("p (h o) -> p h o", o=1).to_broadcast([P, NH, HD]),
                                                ALU.mult).then_inc(s_att, 1)
                run_steps(dve, step, -1, 4, 28, NT, 4)

            @block.tensor
            def _(pe):
                pe.wait_ge(s_const, 9)
                pe.wait_ge(s_w, 64)

                def step(t, u):
                    odd = u % 2 == 1
                    if live(t + 3, NT):
                        pe.wait_ge(s_xn, t + 4)
                        at_least(pe, s_xnT, t + 3)
                        nc.tensor.transpose(ps_xT[:, 0:D], xn[:, (u + 3) % 2, :], ident[:]).then_inc(s_xn_t, 1)
                    if live(t, NT):
                        pe.wait_ge(s_qk, t + 1)
                        pe.wait_ge(s_v, t + 1)
                        z = ps_qkv[u % 2][:, 3 * D:4 * D]
                        if odd:
                            nc.tensor.matmul(z, ones[:], qk[:, u - 1, D:2 * D], start=True, stop=False)
                        nc.tensor.matmul(z, upto[:], qk[:, u, D:2 * D], start=not odd, stop=True).then_inc(s_z, 1)
                        pe.wait_ge(s_kv, t + 1)
                        at_least(pe, s_chain, CH * (t - 2) + 3)
                        for half in range(2):
                            cols = slice(half * 512, (half + 1) * 512)
                            if odd:
                                nc.tensor.matmul(ps_s[1][half][:], ones[:], kv[:, u - 1, cols], start=True, stop=False)
                            ins = nc.tensor.matmul(ps_s[u % 2][half][:], upto[:], kv[:, u, cols],
                                                   start=not odd, stop=True)
                        ins.then_inc(s_s, 1)
                    if live(t - 1, NT):
                        pe.wait_ge(s_att, t)
                        at_least(pe, s_y_out, t - 1)
                        nc.tensor.transpose(ps_o[:, 0:D], att[:, (u + 1) % 2, :], ident[:]).then_inc(s_att_t, 1)
                    if live(t + 2, NT):
                        pe.wait_ge(s_xnT, t + 3)
                        at_least(pe, s_chain, CH * t + 1)
                        nc.tensor.matmul(ps_qkv[u % 2][:, 0:3 * D], ones_bf[:], bias_rows[:, 0:3 * D],
                                         start=True, stop=False)
                        nc.tensor.matmul(ps_qkv[u % 2][:, 0:3 * D], xnT[:, u % 2, :], w_qkv[:],
                                         start=False, stop=True).then_inc(s_qkv, 1)
                    if live(t - 1, NT):
                        pe.wait_ge(s_attT, t)
                        nc.tensor.matmul(ps_o[:, D:2 * D], ones_bf[:], bias_rows[:, 3 * D:4 * D],
                                         start=True, stop=False)
                        nc.tensor.matmul(ps_o[:, D:2 * D], attT[:], w_o[:], start=False, stop=True).then_inc(s_y, 1)
                run_steps(pe, step, -3, 4, 28, NT + 1, 4)

        GT = 4
        GD = GT * D
        rstd2 = sb("rstd2", [P, 2, GT * (NG + 1)])
        nmean2 = sb("nmean2", [P, 2, GT * (NG + 1)])
        stats2 = sb("stats2", [P, 2, GT, 6])
        ya = sb("ya", [P, 2, GD])
        xm = sb("xm", [P, 2, GD])
        xmT = sb("xmT", [P, 2, GD])
        silu_g = sb("silu_g", [P, FC, GD])
        hT = sb("hT", [P, FC, GD])

        s_chain2 = sem("norm_steps2")
        s_norm2 = sem("norms2_ready")
        s_ya = sem("attention_normed")
        s_xm = sem("xm_ready")
        s_xm_t = sem("xm_transposed")
        s_xmT = sem("xmT_ready")
        s_gu = sem("shared_gate_up")
        s_silu = sem("shared_silu")
        s_h = sem("shared_h")
        s_sh = sem("shared_down")
        s_sh_out = sem("shared_stored")
        s_logit = sem("logits_ready")
        s_max = sem("top_found")
        s_router = sem("expert_chosen")

        def tiles(first, count):
            return bass.ds(first, count) if not isinstance(first, int) else slice(first, first + count)

        ps_t2, ps_r, ps_y2 = ps[0], ps[1], ps[2]
        ps_g, ps_u = [ps[3], ps[4]], [ps[5], ps[6]]
        L2 = 17

        with nc.Block() as block:
            @block.scalar
            def _(act):
                def step(s, u):
                    if live(s, NG):
                        for f in range(FC):
                            act.wait_ge(s_gu, 2 * s + 1 + f)
                            at_least(act, s_h, 2 * s - 1 + f)
                            nc.scalar.activation(silu_g[:, f, :], ps_g[f][:], ACT.Silu).then_inc(s_silu, 1)
                    if live(s + 1, NG):
                        act.wait_ge(s_xm_t, s + 2)
                        at_least(act, s_logit, s)
                        nc.scalar.copy(xmT[:, (u + 1) % 2, :], ps_t2[:]).then_inc(s_xmT, 1)
                    if live(s + 2, NG):
                        act.wait_ge(s_norm2, s + 4)
                        at_least(act, s_xm_t, s + 1)
                        for k in range(GT):
                            c = tiles(GT * (s + 3) + k, 1)
                            ins = nc.scalar.activation(
                                xm[:, u % 2, k * D:(k + 1) * D],
                                x_all[:, tiles(GT * (s + 2) + k, 1), :].rearrange("p o d -> p (o d)"),
                                ACT.Identity, bias=nmean2[:, 0, c], scale=rstd2[:, 0, c])
                        ins.then_inc(s_xm, 1)
                    if live(s + 3, NG):
                        act.wait_ge(s_norm2, s + 4)
                        for k in range(GT):
                            c = tiles(GT * (s + 3) + k, 1)
                            ins = nc.scalar.activation(
                                ya[:, (u + 1) % 2, k * D:(k + 1) * D],
                                y_all[:, c, :].rearrange("p o d -> p (o d)"),
                                ACT.Identity, bias=nmean2[:, 1, c], scale=rstd2[:, 1, c])
                        ins.then_inc(s_ya, 1)
                    if live(s, NG):
                        act.wait_ge(s_sh, s + 1)
                        nc.scalar.copy(y_all[:, tiles(GT * s, GT), :].rearrange("p t d -> p (t d)"),
                                       ps_y2[:]).then_inc(s_sh_out, 1)
                run_steps(act, step, -3, 1, 5, NG, 2)

            @block.vector
            def _(dve):
                def step(s, u):
                    first_step = isinstance(s, int) and s == -3
                    link = linker(dve, s_chain2, 0 if first_step else L2 * (s + 3) - 1)
                    if live(s + 2, NG):
                        dve.wait_ge(s_ya, s + 3)
                        xg = x_all[:, tiles(GT * (s + 2), GT), :].rearrange("p t d -> p (t d)")
                        link(nc.vector.tensor_tensor(xg, xg, ya[:, u % 2, :], ALU.add), before_bn_stats=True)
                        for k in range(GT):
                            ins = nc.vector.bn_stats(
                                stats2[:, 0, k, :],
                                x_all[:, tiles(GT * (s + 2) + k, 1), :].rearrange("p o d -> p (o d)"))
                    if live(s + 3, NG):
                        for k in range(GT):
                            ins = nc.vector.bn_stats(
                                stats2[:, 1, k, :],
                                y_all[:, tiles(GT * (s + 3) + k, 1), :].rearrange("p o d -> p (o d)"))
                    kinds = slice(0 if live(s + 2, NG) else 1, 2 if live(s + 3, NG) else 1)
                    if kinds.start < kinds.stop:
                        link(ins)
                        c = tiles(GT * (s + 3), GT)
                        rstd_of(link, [stats2[:, kinds, :, n] for n in range(6)], newton2[:, :, kinds, :], rstd2[:, kinds, c], nmean2[:, kinds, c]).then_inc(s_norm2, 1)
                    if live(s, NG):
                        for f in range(FC):
                            dve.wait_ge(s_silu, 2 * s + 1 + f)
                            at_least(dve, s_sh, s)
                            nc.vector.tensor_tensor(hT[:, f, :], silu_g[:, f, :], ps_u[f][:],
                                                    ALU.mult).then_inc(s_h, 1)
                        dve.wait_ge(s_logit, s + 1)
                        logits = ps_r[:, 0:GT * E].rearrange("p (k e) -> p k e", e=E)
                        c = tiles(GT * s, GT)
                        nc.vector.tensor_reduce(top[:, c], logits, AX, ALU.max).then_inc(s_max, 1)
                        dve.wait_ge(s_max, 3 * s + 1)
                        nc.vector.tensor_tensor(
                            is_top[:], logits,
                            top[:, c].rearrange("p (k o) -> p k o", o=1).to_broadcast([P, GT, E]),
                            ALU.is_equal).then_inc(s_router, 1)
                        dve.wait_ge(s_router, s + 1)
                        nc.vector.tensor_tensor(
                            is_top[:], is_top[:],
                            from_last[:].rearrange("p (o e) -> p o e", o=1).to_broadcast([P, GT, E]),
                            ALU.mult).then_inc(s_max, 1)
                        dve.wait_ge(s_max, 3 * s + 2)
                        nc.vector.tensor_reduce(first_top[:, c], is_top[:], AX, ALU.max).then_inc(s_max, 1)
                dve.wait_ge(s_const, 9)
                run_steps(dve, step, -3, 1, 5, NG, 2)

            @block.tensor
            def _(pe):
                pe.wait_ge(s_w2, 64)

                def step(s, u):
                    if live(s, NG):
                        pe.wait_ge(s_xmT, s + 1)
                        for f in range(FC):
                            at_least(pe, s_h, 2 * s - 1 + f)
                            nc.tensor.matmul(ps_g[f][:], w_g[:, f * P:(f + 1) * P], xmT[:, u % 2, :],
                                             start=True, stop=True)
                            nc.tensor.matmul(ps_u[f][:], w_u[:, f * P:(f + 1) * P], xmT[:, u % 2, :],
                                             start=True, stop=True).then_inc(s_gu, 1)
                    if live(s + 1, NG):
                        pe.wait_ge(s_xm, s + 2)
                        at_least(pe, s_xmT, s + 1)
                        for k in range(GT):
                            ins = nc.tensor.transpose(ps_t2[:, k * P:(k + 1) * P],
                                                      xm[:, (u + 1) % 2, k * D:(k + 1) * D], ident[:])
                        ins.then_inc(s_xm_t, 1)
                    if live(s, NG):
                        at_least(pe, s_router, s)
                        for k in range(GT):
                            ins = nc.tensor.matmul(ps_r[:, k * E:(k + 1) * E], xmT[:, u % 2, k * P:(k + 1) * P],
                                                   w_r[:], start=True, stop=True)
                        ins.then_inc(s_logit, 1)
                        pe.wait_ge(s_h, 2 * s + 2)
                        at_least(pe, s_sh_out, s)
                        for k in range(GT):
                            for f in range(FC):
                                ins = nc.tensor.matmul(ps_y2[:, k * D:(k + 1) * D], hT[:, f, k * P:(k + 1) * P],
                                                       w_d[:, f, :], start=f == 0, stop=f == FC - 1)
                        ins.then_inc(s_sh, 1)
                run_steps(pe, step, -1, 1, 5, NG, 2)

        NE = NT * E
        chosen = sb("chosen", [P, E, NT], BF16)
        counts = sb("counts", [P, E, NT])
        upto_tile = sb("upto_tile", [P, E, NT])
        same_expert = sb("same_expert", [P, E, NT])
        part = sb("part", [P, E], I32)
        padded = sb("padded", [P, E])
        slots_end = sb("slots_end", [P, E])
        slots_base = sb("slots_base", [P, E])
        slot = sb("slot", [P, NT])
        slot_i = sb("slot_i", [P, NT], I32)
        passed = sb("passed", [1, SLOT_TILES, E])
        tile_expert = sb("tile_expert", [1, SLOT_TILES])
        tile_expert_i = sb("tile_expert_i", [1, SLOT_TILES], I32)
        half_tanh = sb("half_tanh", [P, NT])
        score = sb("score", [P, NT])
        rs3 = sb("rs3", [P, NT])
        nm3 = sb("nm3", [P, NT])
        rows = kv[:].rearrange("p a b -> p (a b)").rearrange("p (t d) -> p t d", d=D)

        s_chain3 = sem("slot_steps")
        s_tanh = sem("half_tanh_ready")
        s_chosen = sem("chosen_ready")
        s_ranked = sem("ranks_summed")
        s_score = sem("scales_ready")
        s_rows = sem("rows_ready")
        s_slot = sem("slots_ready")
        s_experts = sem("tile_experts_ready")
        s_scattered = sem("rows_scattered")

        with nc.Block() as block:
            @block.scalar
            def _(act):
                nc.scalar.activation(half_tanh[:], top[:], ACT.Tanh, scale=0.5).then_inc(s_tanh, 1)
                act.wait_ge(s_score, 1)
                with act.Fori(0, NT) as t:
                    c = bass.ds(t, 1)
                    nc.scalar.activation(rows[:, c, :].rearrange("p o d -> p (o d)"),
                                         x_all[:, c, :].rearrange("p o d -> p (o d)"),
                                         ACT.Identity, bias=nm3[:, c], scale=rs3[:, c]).then_inc(s_rows, 1)

            @block.tensor
            def _(pe):
                pe.wait_ge(s_chosen, 1)
                flat = chosen[:].rearrange("p e t -> p (e t)")
                nc.tensor.matmul(ps[0][:], before_bf[:], flat, start=True, stop=True)
                nc.tensor.matmul(ps[1][:], ones_bf[:], flat, start=True, stop=True).then_inc(s_ranked, 1)

            @block.vector
            def _(dve):
                link = linker(dve, s_chain3, 0)
                dve.wait_ge(s_iota, 3)
                nc.vector.tensor_tensor(
                    chosen[:], first_top[:].rearrange("p (o t) -> p o t", o=1).to_broadcast([P, E, NT]),
                    from_last[:].rearrange("p (e o) -> p e o", o=1).to_broadcast([P, E, NT]),
                    ALU.is_equal).then_inc(s_chosen, 1)
                dve.wait_ge(s_tanh, 1)
                link(nc.vector.tensor_scalar(score[:], half_tanh[:], 0.5, 0.5, ALU.mult, ALU.add))
                nc.vector.tensor_tensor(rs3[:], rstd2[:, 0, GT:], score[:], ALU.mult)
                nc.vector.tensor_tensor(nm3[:], nmean2[:, 0, GT:], score[:], ALU.mult).then_inc(s_score, 1)
                link(nc.vector.memset(same_expert[:], 1.0))
                link(nc.vector.memset(same_expert[:, :, 0:1], 0.0))
                dve.wait_ge(s_ranked, 1)
                link(nc.vector.tensor_copy(counts[:].rearrange("p e t -> p (e t)"), ps[1][:]))
                link(nc.vector.tensor_tensor_scan(
                    upto_tile[:].rearrange("p e t -> p (e t)"), same_expert[:].rearrange("p e t -> p (e t)"),
                    counts[:].rearrange("p e t -> p (e t)"), 0.0, ALU.mult, ALU.add))
                total = upto_tile[:, :, NT - 1]
                link(nc.vector.tensor_scalar(part[:], total, float(P - 1), None, ALU.add))
                link(nc.vector.tensor_scalar(part[:], part[:], 7, 7, ALU.logical_shift_right, ALU.logical_shift_left))
                link(nc.vector.tensor_copy(padded[:], part[:]))
                link(nc.vector.tensor_tensor_scan(slots_end[:], ones[:, 0:E], padded[:], 0.0, ALU.mult, ALU.add))
                link(nc.vector.tensor_tensor(slots_base[:], slots_end[:], padded[:], ALU.subtract))
                link(nc.vector.tensor_tensor(counts[:], upto_tile[:], counts[:], ALU.subtract))
                cf = counts[:].rearrange("p e t -> p (e t)")
                link(nc.vector.tensor_tensor(cf, ps[0][:], cf, ALU.add))
                link(nc.vector.tensor_tensor(
                    counts[:], counts[:],
                    slots_base[:].rearrange("p (e o) -> p e o", o=1).to_broadcast([P, E, NT]), ALU.add))
                link(nc.vector.tensor_tensor(counts[:], counts[:], chosen[:], ALU.mult))
                link(nc.vector.tensor_reduce(slot[:], counts[:].rearrange("p e t -> p t e"), AX, ALU.add))
                nc.vector.tensor_copy(slot_i[:], slot[:]).then_inc(s_slot, 1)
                link(nc.vector.tensor_tensor(
                    passed[:], slots_end[0:1, :].rearrange("p (o e) -> p o e", o=1).to_broadcast([1, SLOT_TILES, E]),
                    slot_start[:].rearrange("p (j o) -> p j o", o=1).to_broadcast([1, SLOT_TILES, E]), ALU.is_le))
                link(nc.vector.tensor_reduce(tile_expert[:], passed[:], AX, ALU.add))
                nc.vector.tensor_scalar(tile_expert_i[:], tile_expert[:], float(E - 1), None,
                                        ALU.min).then_inc(s_experts, 1)

            @block.gpsimd
            def _(pool):
                pool.wait_ge(s_slot, 1)
                pool.wait_ge(s_cleared, 16 * SLOT_TILES)
                for t in range(NT):
                    pool.wait_ge(s_rows, t + 1)
                    nc.gpsimd.indirect_dma_start(
                        out=sorted_x, out_offset=bass.IndirectOffsetOnAxis(ap=slot_i[:, t:t + 1], axis=0),
                        in_=rows[:, t, :], in_offset=None).then_inc(s_scattered, 16)
                pool.wait_ge(s_scattered, 16 * NT)

        xs = sb("xs", [P, 4, D])
        xsT = sb("xsT", [P, 2, D])
        silu_e = sb("silu_e", [P, 2, F])
        h_e = sb("h_e", [P, 2, F])
        hT_e = sb("hT_e", [P, 2, F])
        y_e = sb("y_e", [P, 4, D])

        s_load = [sem(f"slots_loaded{i}") for i in range(4)]
        s_store = [sem(f"slots_stored{i}") for i in range(4)]
        s_xs_t = sem("xs_transposed")
        s_xsT = sem("xsT_ready")
        s_gue = sem("expert_gate_up")
        s_silue = sem("expert_silu")
        s_he = sem("expert_h")
        s_he_t = sem("expert_h_transposed")
        s_hTe = sem("expert_hT_ready")
        s_de = sem("expert_down")
        s_ye = sem("expert_y_ready")

        ps_gue = [ps[0], ps[1]]
        ps_xs, ps_h, ps_ye = ps[2], ps[3], ps[4]
        ST = SLOT_TILES

        with nc.Block() as block:
            @block.sync
            def _(sp):
                def step(j, u):
                    if live(j + 6, ST):
                        at_least(sp, s_xs_t, j + 3)
                        sp.dma_start(xs[:, (u + 2) % 4, :],
                                     sorted_x_tiles[:, tiles(j + 6, 1), :].rearrange("p o d -> p (o d)")
                                     ).then_inc(s_load[(u + 2) % 4], 16)
                    if live(j, ST):
                        sp.wait_ge(s_ye, j + 1)
                        sp.dma_start(sorted_y_tiles[:, tiles(j, 1), :].rearrange("p o d -> p (o d)"),
                                     y_e[:, u, :]).then_inc(s_store[u], 16)
                run_steps(sp, step, -6, 4, 40, ST, 4)

            @block.scalar
            def _(act):
                def step(j, u):
                    if live(j + 3, ST):
                        act.wait_ge(s_xs_t, j + 4)
                        at_least(act, s_gue, j + 2)
                        nc.scalar.copy(xsT[:, (u + 1) % 2, :], ps_xs[:, 0:D]).then_inc(s_xsT, 1)
                    if live(j + 2, ST):
                        act.wait_ge(s_gue, j + 3)
                        at_least(act, s_he, j + 1)
                        nc.scalar.activation(silu_e[:, u % 2, :], ps_gue[u % 2][:, 0:F],
                                             ACT.Silu).then_inc(s_silue, 1)
                    if live(j, ST):
                        act.wait_ge(s_de, j + 1)
                        at_least(act, s_store[u], 4 * (j - u))
                        nc.scalar.copy(y_e[:, u, :], ps_ye[:, 0:D]).then_inc(s_ye, 1)
                run_steps(act, step, -3, 4, 44, ST, 4)

            @block.vector
            def _(dve):
                def step(j, u):
                    if live(j, ST):
                        dve.wait_ge(s_he_t, j + 1)
                        at_least(dve, s_de, j - 1)
                        nc.vector.tensor_copy(hT_e[:, u % 2, :], ps_h[:, 0:F]).then_inc(s_hTe, 1)
                    if live(j + 1, ST):
                        dve.wait_ge(s_silue, j + 2)
                        at_least(dve, s_he_t, j)
                        n = (u + 1) % 2
                        nc.vector.tensor_tensor(h_e[:, n, :], silu_e[:, n, :], ps_gue[n][:, F:2 * F],
                                                ALU.mult).then_inc(s_he, 1)
                run_steps(dve, step, -1, 4, 44, ST, 4)

            @block.tensor
            def _(pe):
                pe.wait_ge(s_experts, 1)
                pe.wait_ge(s_wexp, 16 * (E // 4) * (1 + FC))

                def expert(j):
                    return pe.value_load(tile_expert_i[0:1, tiles(j, 1)], min_val=0, max_val=E - 1)

                def step(j, u):
                    if live(j, ST):
                        pe.wait_ge(s_he, j + 1)
                        at_least(pe, s_hTe, j)
                        for c in range(FC):
                            ins = nc.tensor.transpose(ps_h[:, c * P:(c + 1) * P],
                                                      h_e[:, u % 2, c * P:(c + 1) * P], ident[:])
                        ins.then_inc(s_he_t, 1)
                    if live(j + 3, ST):
                        n = (u + 3) % 4
                        pe.wait_ge(s_load[n], 4 * (j + 3 - n) + 16)
                        at_least(pe, s_xsT, j + 3)
                        nc.tensor.transpose(ps_xs[:, 0:D], xs[:, n, :], ident[:]).then_inc(s_xs_t, 1)
                    if live(j + 2, ST):
                        e = expert(j + 2)
                        pe.wait_ge(s_xsT, j + 3)
                        at_least(pe, s_he, j + 1)
                        nc.tensor.matmul(ps_gue[u % 2][:], xsT[:, u % 2, :],
                                         w_exp[:, bass.ds(e, 1), :].rearrange("p o f -> p (o f)"),
                                         start=True, stop=True).then_inc(s_gue, 1)
                    if live(j, ST):
                        e = expert(j)
                        pe.wait_ge(s_hTe, j + 1)
                        at_least(pe, s_ye, j)
                        for c in range(FC):
                            ins = nc.tensor.matmul(
                                ps_ye[:, 0:D], hT_e[:, u % 2, c * P:(c + 1) * P],
                                w_exp_down[:, bass.ds(e, 1), c, :].rearrange("p o d -> p (o d)"),
                                start=c == 0, stop=c == FC - 1)
                        ins.then_inc(s_de, 1)
                run_steps(pe, step, -3, 4, 44, ST, 4)

        rstd5 = sb("rstd5", [P, 2, GT])
        nmean5 = sb("nmean5", [P, 2, GT])

        s_group = [sem(f"group_gathered{i}") for i in range(NG)]
        s_gathered = sem("groups_gathered")
        s_chain5 = sem("norm_steps5")
        s_norm5 = sem("norms5_ready")
        s_yn5 = sem("ffn_normed")
        s_fin = sem("output_ready")
        s_out = sem("output_stored")
        L5 = 17

        with nc.Block() as block:
            @block.gpsimd
            def _(pool):
                for n in range(4):
                    pool.wait_ge(s_store[n], 16 * len(range(n, ST, 4)))
                for t in range(NT):
                    nc.gpsimd.indirect_dma_start(
                        out=rows[:, t, :], out_offset=None,
                        in_=sorted_y, in_offset=bass.IndirectOffsetOnAxis(ap=slot_i[:, t:t + 1], axis=0)
                    ).then_inc(s_group[t // GT], 16)
                for g in range(NG):
                    pool.wait_ge(s_group[g], 16 * GT)
                    pool.sem_inc(s_gathered, 1)

            @block.vector
            def _(dve):
                def step(g, u):
                    link = linker(dve, s_chain5, L5 * g)
                    if live(g, NG):
                        dve.wait_ge(s_gathered, g + 1)
                        yg = rows[:, tiles(GT * g, GT), :].rearrange("p t d -> p (t d)")
                        link(nc.vector.tensor_tensor(
                            yg, yg, y_all[:, tiles(GT * g, GT), :].rearrange("p t d -> p (t d)"), ALU.add),
                            before_bn_stats=True)
                        for k in range(GT):
                            ins = nc.vector.bn_stats(stats2[:, 0, k, :],
                                                     rows[:, tiles(GT * g + k, 1), :].rearrange("p o d -> p (o d)"))
                        link(ins)
                        at_least(dve, s_yn5, g - 1)
                        rstd_of(link, [stats2[:, 0, :, n] for n in range(6)], newton2[:, :, 0, :],
                                rstd5[:, u, :], nmean5[:, u, :]).then_inc(s_norm5, 1)
                    if live(g - 1, NG):
                        dve.wait_ge(s_yn5, g)
                        xg = x_all[:, tiles(GT * (g - 1), GT), :].rearrange("p t d -> p (t d)")
                        nc.vector.tensor_tensor(xg, xg, ya[:, 1 - u, :], ALU.add).then_inc(s_fin, 1)
                run_steps(dve, step, 0, 1, 7, NG + 1, 2)

            @block.scalar
            def _(act):
                def step(g, u):
                    act.wait_ge(s_norm5, g + 1)
                    at_least(act, s_fin, g - 1)
                    for k in range(GT):
                        ins = nc.scalar.activation(ya[:, u, k * D:(k + 1) * D],
                                                   rows[:, tiles(GT * g + k, 1), :].rearrange("p o d -> p (o d)"),
                                                   ACT.Identity, bias=nmean5[:, u, k:k + 1], scale=rstd5[:, u, k:k + 1])
                    ins.then_inc(s_yn5, 1)
                run_steps(act, step, 0, 2, 8, NG, 2)

            @block.sync
            def _(sp):
                for g in range(NG):
                    sp.wait_ge(s_fin, g + 1)
                    sp.dma_start(out_dram[:, GT * g:GT * g + GT, :], x_all[:, GT * g:GT * g + GT, :]).then_inc(s_out, 16)
                sp.wait_ge(s_out, 16 * NG)


_INS = ["x", "wq", "wk", "wv", "wo", "bq", "bk", "bv", "bo", "w_router_t", "gate_up", "down",
        "w_gate_t", "w_up_t", "w_down_t"]


def kernel(**inputs):
    import numpy as np
    import concourse.bacc as bacc
    from concourse.bass_utils import run_bass_kernel_spmd

    given = {n: np.asarray(a) for n, a in inputs.items()}
    laid = {
        "x": given["L0_attn_x"],
        "wq": given["L0_attn_Wq"], "wk": given["L0_attn_Wk"], "wv": given["L0_attn_Wv"], "wo": given["L0_attn_Wo"],
        "bq": given["L0_attn_bq"], "bk": given["L0_attn_bk"], "bv": given["L0_attn_bv"], "bo": given["L0_attn_bo"],
        "w_router_t": given["L0_ffn_w_router"].T, "gate_up": given["L0_ffn_gate_up_proj"],
        "down": given["L0_ffn_down_proj"], "w_gate_t": given["L0_ffn_w_gate"].T,
        "w_up_t": given["L0_ffn_w_up"].T, "w_down_t": given["L0_ffn_w_down"].T,
    }
    nc = bacc.Bacc("TRN2", target_bir_lowering=False, num_devices=1)
    arrays, args = {}, []
    for name in _INS:
        a = np.ascontiguousarray(laid[name])
        arrays[f"in_{name}"] = a
        args.append(nc.dram_tensor(f"in_{name}", a.shape, mybir.dt.from_np(a.dtype), kind="ExternalInput").ap())
    out = nc.dram_tensor("out_0", laid["x"].shape, F32, kind="ExternalOutput").ap()
    build(nc, *args, out)
    r = run_bass_kernel_spmd(nc, [arrays], core_ids=[0])
    return r.results[0]["out_0"]
```

```python
from contextlib import ExitStack

import concourse.bass as bass
from concourse import mybir

F32 = mybir.dt.float32
BF16 = mybir.dt.bfloat16
I32 = mybir.dt.int32
U32 = mybir.dt.uint32
ALU = mybir.AluOpType
ACT = mybir.ActivationFunctionType
AX = mybir.AxisListType.X

P = 128
EPS = 1e-5
EPS_DEN = 1e-6
RSQRT_MAGIC = float(0x5F3759DF)


def live(index, count):
    return not isinstance(index, int) or 0 <= index < count


def at_least(eng, sem, count):
    if not isinstance(count, int) or count > 0:
        eng.wait_ge(sem, count)


def run_steps(eng, body, first, lo, hi, last, unroll):
    assert (hi - lo) % unroll == 0
    for s in range(first, lo):
        body(s, s % unroll)
    with eng.Fori(0, (hi - lo) // unroll) as i:
        for u in range(lo, lo + unroll):
            body(i * unroll + u, u % unroll)
    for s in range(hi, last):
        body(s, s % unroll)


def run_quads(eng, body, first, lo, hi, last):
    for q in range(first, lo):
        for k in range(4):
            body(q, k)
    with eng.Fori(0, hi - lo) as i:
        for k in range(4):
            body(i + lo, k)
    for q in range(hi, last):
        for k in range(4):
            body(q, k)


def tiles(first, count=1):
    return bass.ds(first, count) if not isinstance(first, int) else slice(first, first + count)


def flat(ap):
    return ap.rearrange("p a b -> p (a b)")


class Series:

    def __init__(self, eng, sem, base):
        self.eng, self.sem, self.count = eng, sem, base

    def done(self, ins):
        ins.then_inc(self.sem, 1)
        self.count = self.count + 1

    def wait(self):
        at_least(self.eng, self.sem, self.count)


def rstd_steps(nc, series, st, width, scratch, rs, nm):
    mean_even, sq_even, mean_odd, sq_odd = st[1], st[2], st[4], st[5]
    ve, y, t, mean2 = scratch
    tensor, scalar, fused = nc.vector.tensor_tensor, nc.vector.tensor_scalar, nc.vector.scalar_tensor_tensor
    series.wait()
    yield series.done(tensor(t, mean_even, mean_odd, ALU.subtract))
    yield series.done(tensor(ve, sq_even, sq_odd, ALU.add))
    yield series.done(tensor(mean2, mean_even, mean_odd, ALU.add))
    series.wait()
    yield series.done(scalar(ve, ve, 1.0 / width, EPS, ALU.mult, ALU.add))
    yield series.done(fused(out=t, in0=t, scalar=0.25, in1=t, op0=ALU.mult, op1=ALU.mult))
    series.wait()
    yield series.done(tensor(ve, ve, t, ALU.add))
    series.wait()
    yield series.done(scalar(t.bitcast(I32), ve.bitcast(I32), 1, None, ALU.logical_shift_right))
    series.wait()
    yield series.done(scalar(y.bitcast(I32), t.bitcast(I32), -1.0, RSQRT_MAGIC, ALU.mult, ALU.add))
    for k in range(3):
        series.wait()
        yield series.done(tensor(t, y, y, ALU.mult))
        series.wait()
        yield series.done(fused(out=t, in0=t, scalar=-0.5, in1=ve, op0=ALU.mult, op1=ALU.mult))
        series.wait()
        yield series.done(fused(out=rs if k == 2 else y, in0=t, scalar=1.5, in1=y, op0=ALU.add, op1=ALU.mult))
    series.wait()
    yield fused(out=nm, in0=mean2, scalar=-0.5, in1=rs, op0=ALU.mult, op1=ALU.mult)


RSTD_STEPS = 17
ALLOC_STEPS = 18


def finish(steps):
    for ins in steps:
        pass
    return ins


def build(nc, x, wq, wk, wv, wo, bq, bk, bv, bo, w_router_t, gate_up, down, w_gate_t, w_up_t, w_down_t, out):
    B, S, D = x.shape
    NH = 16
    HD = D // NH
    E = w_router_t.shape[1]
    F = w_gate_t.shape[1]
    FC = F // P
    NTOK = B * S
    NT = NTOK // P
    TPB = S // P
    ST = (NTOK + E * (P - 1)) // P
    GT = 4
    NG = NT // GT
    QUADS = -(-ST // 4)
    GD = GT * D
    KVW = NH * HD * HD
    assert D == P and TPB == 2 and NT % GT == 0

    RW = 2 * D + 4
    SCALE, SHIFT, TOKEN = 2 * D, 2 * D + 1, 2 * D + 2

    x_dram = x.rearrange("b s d -> (b s) d").rearrange("(t p) d -> p t d", p=P)
    out_rows = out.rearrange("b s d -> (b s) d")
    sorted_rows = nc.dram_tensor("sorted_rows", (ST * P, RW), F32, kind="Internal").ap()
    sorted_tiles = sorted_rows.rearrange("(j p) d -> p j d", p=P)
    cleared_rows = sorted_rows.rearrange("(p j) d -> p j d", p=P)

    with ExitStack() as ctx:
        def sb(name, shape, dt=F32):
            return ctx.enter_context(nc.sbuf_tensor(name, shape, dt))

        def sem(name):
            return ctx.enter_context(nc.semaphore(name))

        col_index = sb("col_index", [P, P])
        row_index = sb("row_index", [P, 1])
        row_start = sb("row_start", [P, 1])
        ident = sb("ident", [P, P])
        upto = sb("upto", [P, P])
        ones = sb("ones", [P, P])
        before_bf = sb("before_bf", [P, P], BF16)
        ones_bf = sb("ones_bf", [P, P], BF16)
        from_last = sb("from_last", [P, E])
        wait_taker = sb("wait_taker", [P, 1])
        w_qkv = sb("w_qkv", [P, 3 * D])
        w_o = sb("w_o", [P, D])
        w_r = sb("w_r", [P, E])
        w_g = sb("w_g", [P, F])
        w_u = sb("w_u", [P, F])
        w_d = sb("w_d", [P, FC, D])
        w_exp = sb("w_exp", [P, E, 2 * F])
        w_exp_down = sb("w_exp_down", [P, E, FC, D])
        bias = sb("bias", [P, 4 * D])
        bias_left = sb("bias_left", [P, 4 * D])
        bias_part = sb("bias_part", [P, 3, 4 * D], BF16)
        bias_rows = sb("bias_rows", [P, 4 * D], BF16)
        rows = sb("rows", [P, ST, RW])
        stats = sb("stats", [P, NT, 6])
        rs1 = sb("rs1", [P, NT])
        nm1 = sb("nm1", [P, NT])
        scratch1 = sb("scratch1", [P, 4, NT])
        xn = sb("xn", [P, 2, D])
        xnT = sb("xnT", [P, 2, D])
        ex = sb("ex", [P, 2, 2 * D])
        rl = sb("rl", [P, 2, 2 * D])
        qk = sb("qk", [P, 4, 2 * D])
        vv = sb("vv", [P, 2, D])
        kv = sb("kv", [P, 4, KVW])
        zq = sb("zq", [P, D])
        den = sb("den", [P, NH])
        rden = sb("rden", [P, NH])
        prod = sb("prod", [P, KVW])
        num = sb("num", [P, D])
        att = sb("att", [P, 2, D])
        attT = sb("attT", [P, D])
        rstd2 = sb("rstd2", [P, 2, GT * (NG + 1)])
        nmean2 = sb("nmean2", [P, 2, GT * (NG + 1)])
        stats2 = sb("stats2", [P, 2, GT, 6])
        scratch2 = sb("scratch2", [P, 4, 2, GT])
        ya = sb("ya", [P, 2, GD])
        xm = sb("xm", [P, 2, GD])
        xmT = sb("xmT", [P, 2, GD])
        silu_g = sb("silu_g", [P, FC, GD])
        hT = sb("hT", [P, FC, GD])
        top = sb("top", [P, 2, GT])
        first_top = sb("first_top", [P, GT])
        is_top = sb("is_top", [P, GT, E])
        chosen = sb("chosen", [P, 2, GT, E], BF16)
        half_tanh = sb("half_tanh", [P, GT])
        score = sb("score", [P, 2, GT])
        taken = sb("taken", [P, 2, E])
        room = sb("room", [P, 2, E])
        shift = sb("shift", [P, 2, E])
        ends = sb("ends", [P, 2, E])
        need = sb("need", [P, E], I32)
        grown = sb("grown", [P, E])
        given = sb("given", [P, E])
        shift_new = sb("shift_new", [P, E])
        shift_gain = sb("shift_gain", [P, E])
        room_left = sb("room_left", [P, E])
        shift_taken = sb("shift_taken", [P, E])
        moved = sb("moved", [P, E])
        in_new = sb("in_new", [P, GT, E])
        slot_of = sb("slot_of", [P, GT, E])
        slot = sb("slot", [P, GT])
        slot_i = sb("slot_i", [P, NT], I32)
        all_ends = sb("all_ends", [P, NG, E])
        passed = sb("passed", [P, NG, E])
        tile_rank = sb("tile_rank", [P, 1])
        tile_expert = sb("tile_expert", [1, P], I32)
        xs = sb("xs", [P, 2, D])
        xsT = sb("xsT", [P, 2, D])
        w_now = sb("w_now", [P, 2, 2 * F])
        silu_e = sb("silu_e", [P, 2, F])
        hT_e = sb("hT_e", [P, 2, F])
        stats3 = sb("stats3", [P, 4, 6])
        scratch3 = sb("scratch3", [P, 4, 4])
        rstd3 = sb("rstd3", [P, 4])
        nmean3 = sb("nmean3", [P, 4])
        yn = sb("yn", [P, 2, D])
        token_i = sb("token_i", [P, ST], I32)

        bank = [ctx.enter_context(nc.psum_tensor(f"bank{i}", [P, 512], F32)) for i in range(8)]

        CHUNKS = [(0, 4), (4, 12), (12, NT)]
        s_x = [sem(f"x_loaded{i}") for i in range(len(CHUNKS))]
        s_w = sem("attention_weights_loaded")
        s_bias = sem("bias_loaded")
        s_w2 = sem("ffn_weights_loaded")
        s_wexp = sem("expert_weights_loaded")
        s_iota = sem("indices_written")
        s_const = sem("constants_written")
        s_zero = sem("zeros_written")
        s_cleared = sem("sorted_rows_cleared")
        s_setup = sem("setup_steps")
        s_norm1 = sem("norm1_ready")
        s_xn = sem("xn_ready")
        s_xn_t = sem("xn_transposed")
        s_xnT = sem("xnT_ready")
        s_qkv = sem("qkv_projected")
        s_elu = sem("elu_halves_ready")
        s_v = sem("v_ready")
        s_qk = sem("qk_ready")
        s_kv = sem("kv_ready")
        s_z = sem("z_summed")
        s_s = sem("state_summed")
        s_chain = sem("attention_steps")
        s_att = sem("att_ready")
        s_att_t = sem("att_transposed")
        s_attT = sem("attT_ready")
        s_y = sem("y_projected")
        s_y_out = sem("y_stored")

        s_series2 = sem("norm_steps2")
        s_norm2 = sem("norms2_ready")
        s_x1 = sem("residual_added")
        s_ya = sem("attention_normed")
        s_xm = sem("xm_ready")
        s_xm_t = sem("xm_transposed")
        s_xmT = sem("xmT_ready")
        s_gu = sem("shared_gate_up")
        s_silu = sem("shared_silu")
        s_h = sem("shared_h")
        s_sh = sem("shared_down")
        s_sh_out = sem("shared_stored")
        s_logit = sem("logits_ready")
        s_top = sem("top_found")
        s_route = sem("routing_steps")
        s_chosen = sem("expert_chosen")
        s_rank = sem("ranks_counted")
        s_alloc = sem("allocation_steps")
        s_slot = sem("slots_ready")
        s_tanh = sem("half_tanh_ready")
        s_score = sem("score_ready")
        s_scale = sem("scales_ready")
        s_scattered = sem("rows_scattered")
        s_tile_rank = sem("tile_ranks_ready")
        s_tile_row = sem("tile_ranks_turned")
        s_experts = sem("tile_experts_ready")

        s_quad = [sem(f"quad_loaded{i}") for i in range(4)]
        s_loaded = sem("slot_quads_loaded")
        s_xs = sem("xs_ready")
        s_xs_t = sem("xs_transposed")
        s_xsT = sem("xsT_ready")
        s_wn = sem("expert_weights_copied")
        s_gue = sem("expert_gate_up")
        s_silue = sem("expert_silu")
        s_he = sem("expert_h_ready")
        s_de = sem("expert_down")
        s_sum = sem("ffn_summed")
        s_stats3 = sem("ffn_stats_ready")
        s_series3 = sem("norm_steps3")
        s_yn = sem("ffn_normed")
        s_fin = sem("output_ready")
        s_out = sem("output_stored")

        CH = 6
        SN = RSTD_STEPS + 1
        SQ = RSTD_STEPS + 1

        ps_qkv = [bank[0], bank[1]]
        ps_s = [(bank[2], bank[3]), (bank[4], bank[5])]
        ps_xT, ps_o = bank[6], bank[7]
        ps_t2, ps_r, ps_y2, ps_rank = bank[6], bank[0], bank[1], bank[7]
        ps_g, ps_u = [bank[2], bank[3]], [bank[4], bank[5]]
        ps_gue, ps_ye, ps_xs = [bank[2], bank[3]], [bank[0], bank[1]], bank[6]
        ps_turn = bank[5]

        block = ctx.enter_context(nc.Block())

        @block.sync
        def _(sp):
            for c, (t0, t1) in enumerate(CHUNKS):
                sp.dma_start(rows[:, t0:t1, 0:D], x_dram[:, t0:t1, :]).then_inc(s_x[c], 16)
                if c == 0:
                    for n, w in enumerate((wq, wk, wv)):
                        sp.dma_start(w_qkv[:, n * D:(n + 1) * D], w).then_inc(s_w, 16)
                    sp.dma_start(w_o[:], wo).then_inc(s_w, 16)
            sp.dma_start(w_r[:], w_router_t).then_inc(s_w2, 16)
            sp.dma_start(w_g[:], w_gate_t).then_inc(s_w2, 16)
            sp.dma_start(w_u[:], w_up_t).then_inc(s_w2, 16)
            sp.dma_start(w_d[:], w_down_t.rearrange("(c f) h -> f c h", f=P)).then_inc(s_w2, 16)
            sp.wait_ge(s_zero, 1)
            for j in range(0, ST, ST - NT):
                n = min(ST - NT, ST - j)
                sp.dma_start(cleared_rows[:, j:j + n, :], rows[:, NT:NT + n, :]).then_inc(s_cleared, 16)
            for e in range(0, E, 4):
                sp.dma_start(w_exp[:, e:e + 4, :],
                             gate_up[e:e + 4].rearrange("e h f -> h e f")).then_inc(s_wexp, 16)
                for c in range(FC):
                    sp.dma_start(w_exp_down[:, e:e + 4, c, :],
                                 down[e:e + 4, c * P:(c + 1) * P].rearrange("e f h -> f e h")).then_inc(s_wexp, 16)
            sp.wait_ge(s_scattered, 16 * NT)
            quads = [(q, min(q + 4, ST)) for q in range(0, ST, 4)]
            for n, (j0, j1) in enumerate(quads):
                if n >= 4:
                    sp.wait_ge(s_quad[n % 4], 16 * (n // 4))
                    sp.sem_inc(s_loaded, 1)
                sp.dma_start(rows[:, j0:j1, :], sorted_tiles[:, j0:j1, :]).then_inc(s_quad[n % 4], 16)
            for n in range(len(quads), len(quads) + 4):
                sp.wait_ge(s_quad[n % 4], 16 * (n // 4))
                sp.sem_inc(s_loaded, 1)

        @block.gpsimd
        def _(pool):
            for n, b in enumerate((bq, bk, bv, bo)):
                pool.dma_start(bias[:, n * D:(n + 1) * D],
                               b.rearrange("(o d) -> o d", o=1).to_broadcast([P, D])).then_inc(s_bias, 16)
            whole = dict(allow_small_or_imprecise_dtypes=True)
            nc.gpsimd.iota(col_index[:], [[1, P]], 0, 0, **whole).then_inc(s_iota, 1)
            nc.gpsimd.iota(row_index[:], [[0, 1]], 0, 1, **whole).then_inc(s_iota, 1)
            nc.gpsimd.iota(row_start[:], [[0, 1]], 0, P, **whole).then_inc(s_iota, 1)
            nc.gpsimd.memset(rows[:, NT:ST, :], 0.0).then_inc(s_zero, 1)
            nc.gpsimd.iota(rows[:, 0:NT, TOKEN], [[-P, NT]], NTOK, -1, **whole)
            nc.gpsimd.memset(rows[:, 0:NT, TOKEN + 1], 0.0)

            def step1(t, u):
                pool.wait_ge(s_qk, t + 1)
                pool.wait_ge(s_v, t + 1)
                at_least(pool, s_s, t - 2)
                k = qk[:, u, D:2 * D].rearrange("p (h o d) -> p h o d", h=NH, o=1).to_broadcast([P, NH, HD, HD])
                v = vv[:, u % 2, :].rearrange("p (h m o) -> p h m o", h=NH, o=1).to_broadcast([P, NH, HD, HD])
                nc.gpsimd.tensor_tensor(kv[:, u, :].rearrange("p (h m d) -> p h m d", h=NH, m=HD),
                                        k, v, ALU.mult).then_inc(s_kv, 1)
            run_steps(pool, step1, 0, 4, NT, NT, 4)

            for g in range(NG):
                u = g % 2
                own = slice(GT * g, GT * (g + 1))
                pool.wait_ge(s_tanh, g + 1)
                nc.gpsimd.tensor_scalar(score[:, u, :], half_tanh[:], 0.5, 0.5,
                                        ALU.mult, ALU.add).then_inc(s_score, 1)
                pool.wait_ge(s_score, g + 1)
                pos = slice(GT * (g + 1), GT * (g + 2))
                nc.gpsimd.tensor_tensor(rows[:, own, SCALE], rstd2[:, 0, pos], score[:, u, :],
                                        ALU.mult).then_inc(s_scale, 1)
                nc.gpsimd.tensor_tensor(rows[:, own, SHIFT], nmean2[:, 0, pos], score[:, u, :],
                                        ALU.mult).then_inc(s_scale, 1)
                pool.wait_ge(s_scale, 2 * g + 2)
                pool.wait_ge(s_sh_out, g + 1)
                pool.wait_ge(s_slot, g + 1)
                if g == 0:
                    pool.wait_ge(s_cleared, 16 * len(range(0, ST, ST - NT)))
                for t in range(GT * g, GT * (g + 1)):
                    nc.gpsimd.indirect_dma_start(
                        out=sorted_rows, out_offset=bass.IndirectOffsetOnAxis(ap=slot_i[:, t:t + 1], axis=0),
                        in_=rows[:, t, :], in_offset=None).then_inc(s_scattered, 16)

            for j in range(ST):
                pool.wait_ge(s_fin, j + 1)
                nc.gpsimd.indirect_dma_start(
                    out=out_rows, out_offset=bass.IndirectOffsetOnAxis(ap=token_i[:, j:j + 1], axis=0),
                    in_=rows[:, j, 0:D], in_offset=None,
                    bounds_check=NTOK - 1, oob_is_err=False).then_inc(s_out, 16)
            pool.wait_ge(s_out, 16 * ST)

        @block.scalar
        def _(act):
            def step1(t, u):
                if live(t + 4, NT):
                    at = t + 4
                    act.wait_ge(s_norm1, len(CHUNKS) if not isinstance(t, int) else
                                1 + max(c for c, (t0, _) in enumerate(CHUNKS) if t0 <= at))
                    at_least(act, s_xn_t, t + 3)
                    nc.scalar.activation(xn[:, u % 2, :], flat(rows[:, tiles(at), 0:D]), ACT.Identity,
                                         bias=nm1[:, tiles(at)], scale=rs1[:, tiles(at)]).then_inc(s_xn, 1)
                if live(t + 3, NT):
                    act.wait_ge(s_xn_t, t + 4)
                    at_least(act, s_qkv, t + 2)
                    nc.scalar.copy(xnT[:, (u + 3) % 2, :], ps_xT[:, 0:D]).then_inc(s_xnT, 1)
                if live(t - 1, NT):
                    act.wait_ge(s_att_t, t)
                    at_least(act, s_y, t - 1)
                    nc.scalar.copy(attT[:], ps_o[:, 0:D]).then_inc(s_attT, 1)
                if live(t + 2, NT):
                    act.wait_ge(s_qkv, t + 3)
                    at_least(act, s_qk, t + 1)
                    nc.scalar.activation(ex[:, u % 2, :], ps_qkv[u % 2][:, 0:2 * D], ACT.Exp).then_inc(s_elu, 1)
                    nc.scalar.activation(rl[:, u % 2, :], ps_qkv[u % 2][:, 0:2 * D], ACT.Relu).then_inc(s_elu, 1)
                    at_least(act, s_kv, t + 1)
                    nc.scalar.copy(vv[:, u % 2, :], ps_qkv[u % 2][:, 2 * D:3 * D]).then_inc(s_v, 1)
                if live(t - 1, NT):
                    act.wait_ge(s_y, t)
                    nc.scalar.copy(flat(rows[:, tiles(t - 1), D:2 * D]), ps_o[:, D:2 * D]).then_inc(s_y_out, 1)

            def step2(s, u):
                if live(s, NG):
                    for f in range(FC):
                        act.wait_ge(s_gu, 2 * s + 1 + f)
                        at_least(act, s_h, 2 * s - 1 + f)
                        nc.scalar.activation(silu_g[:, f, :], ps_g[f][:], ACT.Silu).then_inc(s_silu, 1)
                if live(s + 1, NG):
                    act.wait_ge(s_xm_t, s + 2)
                    at_least(act, s_logit, s)
                    nc.scalar.copy(xmT[:, (u + 1) % 2, :], ps_t2[:]).then_inc(s_xmT, 1)
                if live(s + 3, NG):
                    act.wait_ge(s_norm2, s + 4)
                    for k in range(GT):
                        c = tiles(GT * (s + 3) + k)
                        ins = nc.scalar.activation(
                            ya[:, (u + 1) % 2, k * D:(k + 1) * D], flat(rows[:, c, D:2 * D]),
                            ACT.Identity, bias=nmean2[:, 1, c], scale=rstd2[:, 1, c])
                    ins.then_inc(s_ya, 1)
                if live(s + 2, NG):
                    act.wait_ge(s_norm2, s + 4)
                    at_least(act, s_xm_t, s + 1)
                    for k in range(GT):
                        c = tiles(GT * (s + 3) + k)
                        ins = nc.scalar.activation(
                            xm[:, u % 2, k * D:(k + 1) * D], flat(rows[:, tiles(GT * (s + 2) + k), 0:D]),
                            ACT.Identity, bias=nmean2[:, 0, c], scale=rstd2[:, 0, c])
                    ins.then_inc(s_xm, 1)
                if live(s, NG):
                    act.wait_ge(s_top, s + 1)
                    at_least(act, s_score, s)
                    nc.scalar.activation(half_tanh[:], top[:, u, :], ACT.Tanh, scale=0.5).then_inc(s_tanh, 1)
                    act.wait_ge(s_sh, s + 1)
                    nc.scalar.copy(rows[:, tiles(GT * s, GT), D:2 * D],
                                   ps_y2[:].rearrange("p (t d) -> p t d", d=D)).then_inc(s_sh_out, 1)

            run_steps(act, step1, -4, 4, 28, NT - 1, 4)
            step2(-3, 1)
            step1(NT - 1, 3)
            step2(-2, 0)
            step1(NT, 0)
            run_steps(act, step2, -1, 1, 5, NG, 2)

            act.wait_ge(s_experts, 1)
            act.wait_ge(s_wexp, 16 * (E // 4) * (1 + FC))

            def step3(q, u):
                j = 4 * q + u
                if live(j + 4, ST):
                    if u == 0:
                        act.wait_ge(s_loaded, q + 2)
                    at_least(act, s_xs_t, j + 3)
                    r = rows[:, tiles(j + 4), :]
                    nc.scalar.activation(xs[:, u % 2, :], flat(r[:, :, 0:D]), ACT.Identity,
                                         bias=flat(r[:, :, SHIFT:SHIFT + 1]),
                                         scale=flat(r[:, :, SCALE:SCALE + 1])).then_inc(s_xs, 1)
                if live(j + 3, ST):
                    act.wait_ge(s_xs_t, j + 4)
                    at_least(act, s_gue, j + 2)
                    nc.scalar.copy(xsT[:, (u + 1) % 2, :], ps_xs[:, 0:D]).then_inc(s_xsT, 1)
                if live(j + 2, ST):
                    act.wait_ge(s_gue, j + 3)
                    at_least(act, s_he, j + 1)
                    nc.scalar.activation(silu_e[:, u % 2, :], ps_gue[u % 2][:, 0:F], ACT.Silu).then_inc(s_silue, 1)
                if live(j + 4, ST):
                    e = act.value_load(tile_expert[0:1, tiles(j + 4)], min_val=0, max_val=E - 1)
                    nc.scalar.copy(w_now[:, u % 2, :], flat(w_exp[:, bass.ds(e, 1), :])).then_inc(s_wn, 1)
            run_quads(act, step3, -1, 1, 10, 12)

        @block.vector
        def _(dve):
            setup = Series(dve, s_setup, 0)
            dve.wait_ge(s_iota, 2)
            nc.vector.tensor_scalar(ident[:], col_index[:], row_index[:], None, ALU.is_equal).then_inc(s_const, 1)

            def norm_chunk(c):
                t0, t1 = CHUNKS[c]
                r = slice(t0, t1)
                dve.wait_ge(s_x[c], 16)
                for t in range(t0, t1):
                    ins = nc.vector.bn_stats(stats[:, t, :], rows[:, t, 0:D])
                setup.done(ins)
                return rstd_steps(nc, setup, [stats[:, r, n] for n in range(6)], D,
                                  [scratch1[:, n, r] for n in range(4)], rs1[:, r], nm1[:, r])

            first = norm_chunk(0)
            next(first), next(first), next(first)
            nc.vector.memset(ones[:], 1.0).then_inc(s_const, 1)
            next(first)
            nc.vector.memset(ones_bf[:], 1.0).then_inc(s_const, 1)
            next(first)
            setup.done(nc.vector.memset(bias_rows[:], 0.0))
            next(first), next(first)
            nc.vector.tensor_scalar(upto[:], col_index[:], row_index[:], None, ALU.is_ge).then_inc(s_const, 1)
            finish(first).then_inc(s_norm1, 1)
            nc.vector.tensor_scalar(before_bf[:], col_index[:], row_index[:], None, ALU.is_gt).then_inc(s_const, 1)
            nc.vector.tensor_scalar(from_last[:], col_index[:, 0:E], -1.0, float(E),
                                    ALU.mult, ALU.add).then_inc(s_const, 1)
            nc.vector.memset(taken[:, 1, :], 0.0)
            nc.vector.memset(room[:, 1, :], 0.0)
            nc.vector.memset(shift[:, 1, :], 0.0)
            nc.vector.memset(ends[:, 1, :], 0.0).then_inc(s_const, 1)
            dve.wait_ge(s_bias, 64)
            for n in range(3):
                src = bias if n == 0 else bias_left
                setup.done(nc.vector.tensor_copy(bias_part[:, n, :], src[:]))
                setup.wait()
                nc.vector.tensor_copy(bias_rows[32 * n:32 * n + 1, :],
                                      bias_part[32 * n:32 * n + 1, n, :]).then_inc(s_const, 1)
                if n < 2:
                    setup.done(nc.vector.tensor_tensor(bias_left[:], src[:], bias_part[:, n, :], ALU.subtract))
                    setup.wait()

            def step1(t, u):
                if live(t, NT):
                    dve.wait_ge(s_z, t + 1)
                    at_least(dve, s_chain, CH * t)
                    q = qk[:, u, 0:D]
                    nc.vector.tensor_tensor(zq[:], ps_qkv[u % 2][:, 3 * D:4 * D], q, ALU.mult).then_inc(s_chain, 1)
                if live(t + 1, NT):
                    dve.wait_ge(s_elu, 2 * (t + 2))
                    n = (u + 1) % 4
                    nc.vector.scalar_tensor_tensor(out=qk[:, n, :], in0=ex[:, n % 2, :], scalar=1.0,
                                                   in1=rl[:, n % 2, :], op0=ALU.min, op1=ALU.add).then_inc(s_qk, 1)
                if live(t, NT):
                    dve.wait_ge(s_chain, CH * t + 1)
                    nc.vector.tensor_reduce(den[:], zq[:].rearrange("p (h d) -> p h d", h=NH), AX,
                                            ALU.add).then_inc(s_chain, 1)
                    dve.wait_ge(s_s, t + 1)
                    for half in range(2):
                        w = KVW // 2
                        qb = qk[:, u, half * D // 2:(half + 1) * D // 2].rearrange(
                            "p (h o d) -> p h o d", h=NH // 2, o=1).to_broadcast([P, NH // 2, HD, HD])
                        ins = nc.vector.tensor_tensor(
                            prod[:, half * w:(half + 1) * w].rearrange("p (h m d) -> p h m d", h=NH // 2, m=HD),
                            ps_s[u % 2][half][:].rearrange("p (h m d) -> p h m d", h=NH // 2, m=HD), qb, ALU.mult)
                    ins.then_inc(s_chain, 1)
                    dve.wait_ge(s_chain, CH * t + 2)
                    nc.vector.tensor_scalar(rden[:], den[:], EPS_DEN, None, ALU.add).then_inc(s_chain, 1)
                    dve.wait_ge(s_chain, CH * t + 3)
                    nc.vector.tensor_reduce(num[:], prod[:].rearrange("p (n d) -> p n d", d=HD), AX,
                                            ALU.add).then_inc(s_chain, 1)
                    dve.wait_ge(s_chain, CH * t + 4)
                    nc.vector.reciprocal(rden[:], rden[:]).then_inc(s_chain, 1)
                    dve.wait_ge(s_chain, CH * t + 6)
                    at_least(dve, s_att_t, t - 1)
                    nc.vector.tensor_tensor(att[:, u % 2, :].rearrange("p (h m) -> p h m", h=NH),
                                            num[:].rearrange("p (h m) -> p h m", h=NH),
                                            rden[:].rearrange("p (h o) -> p h o", o=1).to_broadcast([P, NH, HD]),
                                            ALU.mult).then_inc(s_att, 1)

            def slot_steps(g, u):
                dve.wait_ge(s_rank, g + 1)
                last, now = 1 - u, u
                sr = Series(dve, s_alloc, ALLOC_STEPS * g)
                tensor, scalar, fused = nc.vector.tensor_tensor, nc.vector.tensor_scalar, nc.vector.scalar_tensor_tensor

                def wide(ap):
                    return ap.rearrange("p (o e) -> p o e", o=1).to_broadcast([P, GT, E])
                ranks = ps_rank[:, 0:GT * E].rearrange("p (t e) -> p t e", e=E)
                totals = ps_rank[:, GT * E:(GT + 1) * E]
                yield sr.done(tensor(taken[:, now, :], taken[:, last, :], totals, ALU.add))
                yield sr.done(tensor(room_left[:], room[:, last, :], taken[:, last, :], ALU.subtract))
                yield sr.done(tensor(shift_taken[:], shift[:, last, :], taken[:, last, :], ALU.add))
                sr.wait()
                yield sr.done(fused(out=need[:], in0=taken[:, now, :], scalar=float(P - 1), in1=room[:, last, :],
                                    op0=ALU.add, op1=ALU.subtract))
                yield sr.done(tensor(in_new[:], ranks, wide(room_left[:]), ALU.is_ge))
                yield sr.done(tensor(slot_of[:], ranks, wide(shift_taken[:]), ALU.add))
                sr.wait()
                yield sr.done(scalar(need[:], need[:], 7, 7, ALU.logical_shift_right, ALU.logical_shift_left))
                sr.wait()
                yield sr.done(nc.vector.tensor_copy(grown[:], need[:]))
                sr.wait()
                yield sr.done(nc.vector.tensor_tensor_scan(given[:], ones[:, 0:E], grown[:], 0.0, ALU.mult, ALU.add))
                yield sr.done(tensor(room[:, now, :], room[:, last, :], grown[:], ALU.add))
                sr.wait()
                yield sr.done(scalar(ends[:, now, :], given[:], ends[:, last, E - 1:E], None, ALU.add))
                sr.wait()
                yield sr.done(tensor(shift_new[:], ends[:, now, :], room[:, now, :], ALU.subtract))
                yield nc.vector.tensor_copy(flat(all_ends[:, tiles(g), :]), ends[:, now, :])
                sr.wait()
                yield sr.done(tensor(shift_gain[:], shift_new[:], shift[:, last, :], ALU.subtract))
                sr.wait()
                yield sr.done(tensor(in_new[:], in_new[:], wide(shift_gain[:]), ALU.mult))
                yield sr.done(fused(out=moved[:], in0=grown[:], scalar=0.0, in1=shift_gain[:],
                                    op0=ALU.is_gt, op1=ALU.mult))
                sr.wait()
                yield sr.done(tensor(slot_of[:], slot_of[:], in_new[:], ALU.add))
                yield tensor(shift[:, now, :], shift[:, last, :], moved[:], ALU.add)
                sr.wait()
                yield sr.done(tensor(slot_of[:], slot_of[:], chosen[:, now, :, :], ALU.mult))
                sr.wait()
                yield sr.done(nc.vector.tensor_reduce(slot[:], slot_of[:], AX, ALU.add))
                sr.wait()
                yield nc.vector.tensor_copy(slot_i[:, tiles(GT * g, GT)], slot[:]).then_inc(s_slot, 1)

            def h_and_choice_steps(s, u):
                logits = ps_r[:, 0:GT * E].rearrange("p (k e) -> p k e", e=E)

                def h(f):
                    dve.wait_ge(s_silu, 2 * s + 1 + f)
                    at_least(dve, s_sh, s)
                    return nc.vector.tensor_tensor(hT[:, f, :], silu_g[:, f, :], ps_u[f][:], ALU.mult).then_inc(s_h, 1)
                yield h(0)
                dve.wait_ge(s_logit, s + 1)
                yield nc.vector.tensor_reduce(top[:, u, :], logits, AX, ALU.max).then_inc(s_top, 1)
                yield h(1)
                dve.wait_ge(s_top, s + 1)
                yield nc.vector.tensor_tensor(
                    is_top[:], logits, top[:, u, :].rearrange("p (k o) -> p k o", o=1).to_broadcast([P, GT, E]),
                    ALU.is_equal).then_inc(s_route, 1)
                dve.wait_ge(s_route, 3 * s + 1)
                yield nc.vector.tensor_tensor(
                    is_top[:], is_top[:], from_last[:].rearrange("p (o e) -> p o e", o=1).to_broadcast([P, GT, E]),
                    ALU.mult).then_inc(s_route, 1)
                dve.wait_ge(s_route, 3 * s + 2)
                yield nc.vector.tensor_reduce(first_top[:], is_top[:], AX, ALU.max).then_inc(s_route, 1)
                dve.wait_ge(s_route, 3 * s + 3)
                yield nc.vector.tensor_tensor(
                    chosen[:, u, :, :], is_top[:],
                    first_top[:].rearrange("p (k o) -> p k o", o=1).to_broadcast([P, GT, E]),
                    ALU.is_equal).then_inc(s_chosen, 1)

            def step2(s, u):
                alloc = slot_steps(s - 1, 1 - u) if live(s - 1, NG) else iter(())
                mains = h_and_choice_steps(s, u) if live(s, NG) else iter(())
                norm = Series(dve, s_series2, SN * (s + 3))
                if isinstance(s, int) and s < 0:
                    dve.wait_ge(s_y_out, NT if s == -1 else GT * (s + 4))
                for k in range(GT):
                    if live(s + 3, NG):
                        ins = nc.vector.bn_stats(stats2[:, 1, k, :], flat(rows[:, tiles(GT * (s + 3) + k), D:2 * D]))
                    if k > 1:
                        next(alloc, None)
                if live(s + 2, NG):
                    dve.wait_ge(s_ya, s + 3)
                    xg = rows[:, tiles(GT * (s + 2), GT), 0:D]
                    nc.vector.tensor_tensor(xg, xg, ya[:, u % 2, :].rearrange("p (t d) -> p t d", d=D),
                                            ALU.add).then_inc(s_x1, 1)
                    next(alloc, None)
                    dve.wait_ge(s_x1, s + 3)
                    nc.vector.memset(wait_taker[:], 0.0)
                    for k in range(GT):
                        ins = nc.vector.bn_stats(stats2[:, 0, k, :], flat(rows[:, tiles(GT * (s + 2) + k), 0:D]))
                        if k < GT - 1:
                            next(alloc, None), next(alloc, None)
                kinds = slice(0 if live(s + 2, NG) else 1, 2 if live(s + 3, NG) else 1)
                if kinds.start < kinds.stop:
                    norm.done(ins)
                    c = tiles(GT * (s + 3), GT)
                    norms = rstd_steps(nc, norm, [stats2[:, kinds, :, n] for n in range(6)], D,
                                       [scratch2[:, n, kinds, :] for n in range(4)],
                                       rstd2[:, kinds, c], nmean2[:, kinds, c])
                    for i, ins in enumerate(norms):
                        last = ins
                        next(alloc, None)
                        if i > 3 and i % 2 == 0:
                            next(mains, None)
                    last.then_inc(s_norm2, 1)
                for _ in alloc:
                    next(mains, None)
                for _ in mains:
                    pass

            step1(-1, 3)
            for c in range(1, len(CHUNKS)):
                finish(norm_chunk(c)).then_inc(s_norm1, 1)
                step1(c - 1, c - 1)
            run_steps(dve, step1, len(CHUNKS) - 1, 4, 28, NT - 2, 4)
            step2(-3, 1)
            step1(NT - 2, 2)
            step2(-2, 0)
            step1(NT - 1, 3)
            run_steps(dve, step2, -1, 1, 5, NG + 1, 2)

            dve.wait_ge(s_slot, NG)
            dve.wait_ge(s_iota, 3)
            setup.done(nc.vector.tensor_scalar(flat(passed[:]), flat(all_ends[:]), row_start[:], None, ALU.is_le))
            setup.wait()
            nc.vector.tensor_reduce(tile_rank[:], flat(passed[:]), AX, ALU.add).then_inc(s_tile_rank, 1)
            dve.wait_ge(s_tile_row, 1)
            setup.done(nc.vector.tensor_copy(tile_expert[:], ps_turn[0:1, 0:P]))
            setup.wait()
            nc.vector.tensor_scalar(tile_expert[:], tile_expert[:], E - 1, None, ALU.bitwise_and).then_inc(s_experts, 1)

            norms3 = {}

            def step3(q, u):
                j = 4 * q + u

                def norm_step(count=1):
                    for _ in range(count):
                        next(norms3["steps"], None)

                if u == 0 and live(q - 1, QUADS):
                    n = min(4, ST - 4 * (q - 1)) if isinstance(q, int) else 4
                    norm = Series(dve, s_series3, SQ * (q - 1))
                    norms3["n"] = n
                    norms3["steps"] = norm_quad(q, n, norm)
                elif u == 0:
                    norms3["steps"] = iter(())
                if live(j - 8, ST):
                    i = tiles(j - 8)
                    if u == 0:
                        dve.wait_ge(s_series3, SQ * (q - 1))
                    nc.vector.tensor_scalar(yn[:, u % 2, :], flat(rows[:, i, D:2 * D]), rstd3[:, u:u + 1],
                                            nmean3[:, u:u + 1], ALU.mult, ALU.add).then_inc(s_yn, 1)
                if u:
                    norm_step()
                at_least(dve, s_sum, min(j, ST) if isinstance(j, int) else j)
                if live(j + 2, ST):
                    dve.wait_ge(s_silue, j + 3)
                    at_least(dve, s_de, j + 1)
                    nc.vector.tensor_tensor(hT_e[:, u % 2, :], silu_e[:, u % 2, :], ps_gue[u % 2][:, F:2 * F],
                                            ALU.mult).then_inc(s_he, 1)
                if live(j - 1, ST):
                    nc.vector.bn_stats(stats3[:, (u + 3) % 4, :],
                                       flat(rows[:, tiles(j - 1), D:2 * D])).then_inc(s_stats3, 1)
                norm_step()
                if live(j - 8, ST):
                    dve.wait_ge(s_yn, j - 7)
                    nc.vector.tensor_tensor(flat(rows[:, i, 0:D]), flat(rows[:, i, 0:D]), yn[:, u % 2, :],
                                            ALU.add).then_inc(s_fin, 1)
                norm_step()
                if live(j, ST):
                    r = flat(rows[:, tiles(j), D:2 * D])
                    dve.wait_ge(s_de, j + 1)
                    nc.vector.tensor_tensor(r, ps_ye[u % 2][:, 0:D], r, ALU.add).then_inc(s_sum, 1)
                norm_step()
                if u == 3:
                    norm_step(20)

            def norm_quad(q, n, norm):
                dve.wait_ge(s_stats3, min(4 * q, ST) if isinstance(q, int) else 4 * q)
                for ins in rstd_steps(nc, norm, [stats3[:, 0:n, k] for k in range(6)], D,
                                      [scratch3[:, k, 0:n] for k in range(4)], rstd3[:, 0:n], nmean3[:, 0:n]):
                    last = ins
                    yield ins
                norm.done(last)
                c = tiles(4 * (q - 1), n)
                yield nc.vector.tensor_scalar(token_i[:, c], rows[:, c, TOKEN], -1.0, float(NTOK),
                                              ALU.mult, ALU.add)

            run_quads(dve, step3, -1, 2, 11, QUADS + 2)

        @block.tensor
        def _(pe):
            def step1(t, u):
                odd = u % 2 == 1
                if live(t + 3, NT):
                    pe.wait_ge(s_xn, t + 4)
                    at_least(pe, s_xnT, t + 3)
                    nc.tensor.transpose(ps_xT[:, 0:D], xn[:, (u + 3) % 2, :], ident[:]).then_inc(s_xn_t, 1)
                if live(t, NT):
                    pe.wait_ge(s_qk, t + 1)
                    pe.wait_ge(s_v, t + 1)
                    z = ps_qkv[u % 2][:, 3 * D:4 * D]
                    if odd:
                        nc.tensor.matmul(z, ones[:], qk[:, u - 1, D:2 * D], start=True, stop=False)
                    nc.tensor.matmul(z, upto[:], qk[:, u, D:2 * D], start=not odd, stop=True).then_inc(s_z, 1)
                    pe.wait_ge(s_kv, t + 1)
                    at_least(pe, s_chain, CH * (t - 2) + 3)
                    for half in range(2):
                        cols = slice(half * 512, (half + 1) * 512)
                        if odd:
                            nc.tensor.matmul(ps_s[1][half][:], ones[:], kv[:, u - 1, cols], start=True, stop=False)
                        ins = nc.tensor.matmul(ps_s[u % 2][half][:], upto[:], kv[:, u, cols],
                                               start=not odd, stop=True)
                    ins.then_inc(s_s, 1)
                if live(t - 1, NT):
                    pe.wait_ge(s_att, t)
                    at_least(pe, s_y_out, t - 1)
                    nc.tensor.transpose(ps_o[:, 0:D], att[:, (u + 1) % 2, :], ident[:]).then_inc(s_att_t, 1)
                if live(t + 2, NT):
                    pe.wait_ge(s_xnT, t + 3)
                    if isinstance(t, int) and t == -2:
                        pe.wait_ge(s_const, 10)
                        pe.wait_ge(s_w, 64)
                    at_least(pe, s_chain, CH * t + 1)
                    nc.tensor.matmul(ps_qkv[u % 2][:, 0:3 * D], ones_bf[:], bias_rows[:, 0:3 * D],
                                     start=True, stop=False)
                    nc.tensor.matmul(ps_qkv[u % 2][:, 0:3 * D], xnT[:, u % 2, :], w_qkv[:],
                                     start=False, stop=True).then_inc(s_qkv, 1)
                if live(t - 1, NT):
                    pe.wait_ge(s_attT, t)
                    nc.tensor.matmul(ps_o[:, D:2 * D], ones_bf[:], bias_rows[:, 3 * D:4 * D],
                                     start=True, stop=False)
                    nc.tensor.matmul(ps_o[:, D:2 * D], attT[:], w_o[:], start=False, stop=True).then_inc(s_y, 1)
            pe.wait_ge(s_const, 1)
            run_steps(pe, step1, -3, 4, 28, NT + 1, 4)

            def step2(s, u):
                def gate_up_of(f):
                    if live(s, NG):
                        at_least(pe, s_h, 2 * s - 1 + f)
                        nc.tensor.matmul(ps_g[f][:], w_g[:, f * P:(f + 1) * P], xmT[:, u % 2, :],
                                         start=True, stop=True)
                        nc.tensor.matmul(ps_u[f][:], w_u[:, f * P:(f + 1) * P], xmT[:, u % 2, :],
                                         start=True, stop=True).then_inc(s_gu, 1)

                if live(s, NG):
                    pe.wait_ge(s_xmT, s + 1)
                gate_up_of(0)
                gate_up_of(1)
                if live(s + 1, NG):
                    pe.wait_ge(s_xm, s + 2)
                    at_least(pe, s_xmT, s + 1)
                    for k in range(GT):
                        ins = nc.tensor.transpose(ps_t2[:, k * P:(k + 1) * P],
                                                  xm[:, (u + 1) % 2, k * D:(k + 1) * D], ident[:])
                    ins.then_inc(s_xm_t, 1)
                if live(s, NG):
                    at_least(pe, s_chosen, s)
                    for k in range(GT):
                        ins = nc.tensor.matmul(ps_r[:, k * E:(k + 1) * E], xmT[:, u % 2, k * P:(k + 1) * P],
                                               w_r[:], start=True, stop=True)
                    ins.then_inc(s_logit, 1)
                    pe.wait_ge(s_h, 2 * s + 2)
                    at_least(pe, s_sh_out, s)
                    for k in range(GT):
                        for f in range(FC):
                            ins = nc.tensor.matmul(ps_y2[:, k * D:(k + 1) * D], hT[:, f, k * P:(k + 1) * P],
                                                   w_d[:, f, :], start=f == 0, stop=f == FC - 1)
                    ins.then_inc(s_sh, 1)
                if live(s, NG):
                    n = GT * E
                    pick = chosen[:, u, :, :].rearrange("p k e -> p (k e)")
                    pe.wait_ge(s_chosen, s + 1)
                    nc.tensor.matmul(ps_rank[:, 0:n], before_bf[:], pick, start=True, stop=False)
                    for k in range(1, GT):
                        nc.tensor.matmul(ps_rank[:, k * E:n], ones_bf[:], pick[:, 0:n - k * E],
                                         start=False, stop=k == GT - 1)
                    for k in range(GT):
                        ins = nc.tensor.matmul(ps_rank[:, n:n + E], ones_bf[:], pick[:, k * E:(k + 1) * E],
                                               start=k == 0, stop=k == GT - 1)
                    ins.then_inc(s_rank, 1)
            pe.wait_ge(s_w2, 64)
            pe.wait_ge(s_xnT, NT)
            step2(-1, 1)
            pe.wait_ge(s_chain, CH * NT)
            pe.wait_ge(s_y_out, NT)
            run_steps(pe, step2, 0, 1, 7, NG, 2)

            pe.wait_ge(s_tile_rank, 1)
            nc.tensor.matmul(ps_turn[0:1, 0:P], tile_rank[:], ident[:], start=True, stop=True).then_inc(s_tile_row, 1)

            def step3(q, u):
                j = 4 * q + u
                if live(j + 3, ST):
                    pe.wait_ge(s_xs, j + 4)
                    at_least(pe, s_xsT, j + 3)
                    nc.tensor.transpose(ps_xs[:, 0:D], xs[:, (u + 1) % 2, :], ident[:]).then_inc(s_xs_t, 1)
                if live(j + 2, ST):
                    pe.wait_ge(s_xsT, j + 3)
                    pe.wait_ge(s_wn, j + 3)
                    at_least(pe, s_he, j + 1)
                    for c in range(2 * FC):
                        ins = nc.tensor.matmul(ps_gue[u % 2][:, c * P:(c + 1) * P],
                                               w_now[:, u % 2, c * P:(c + 1) * P], xsT[:, u % 2, :],
                                               start=True, stop=True)
                    ins.then_inc(s_gue, 1)
                if live(j, ST):
                    e = pe.value_load(tile_expert[0:1, tiles(j)], min_val=0, max_val=E - 1)
                    pe.wait_ge(s_he, j + 1)
                    at_least(pe, s_sum, j - 1)
                    for c in range(FC):
                        ins = nc.tensor.matmul(ps_ye[u % 2][:, 0:D], hT_e[:, u % 2, c * P:(c + 1) * P],
                                               flat(w_exp_down[:, bass.ds(e, 1), c, :]),
                                               start=c == 0, stop=c == FC - 1)
                    ins.then_inc(s_de, 1)
            pe.wait_ge(s_experts, 1)
            pe.wait_ge(s_wexp, 16 * (E // 4) * (1 + FC))
            run_quads(pe, step3, -1, 1, 10, QUADS)


_INS = ["x", "wq", "wk", "wv", "wo", "bq", "bk", "bv", "bo", "w_router_t", "gate_up", "down",
        "w_gate_t", "w_up_t", "w_down_t"]


def kernel(**inputs):
    import numpy as np
    import concourse.bacc as bacc
    from concourse.bass_utils import run_bass_kernel_spmd

    given = {n: np.asarray(a) for n, a in inputs.items()}
    laid = {
        "x": given["L0_attn_x"],
        "wq": given["L0_attn_Wq"], "wk": given["L0_attn_Wk"], "wv": given["L0_attn_Wv"], "wo": given["L0_attn_Wo"],
        "bq": given["L0_attn_bq"], "bk": given["L0_attn_bk"], "bv": given["L0_attn_bv"], "bo": given["L0_attn_bo"],
        "w_router_t": given["L0_ffn_w_router"].T, "gate_up": given["L0_ffn_gate_up_proj"],
        "down": given["L0_ffn_down_proj"], "w_gate_t": given["L0_ffn_w_gate"].T,
        "w_up_t": given["L0_ffn_w_up"].T, "w_down_t": given["L0_ffn_w_down"].T,
    }
    nc = bacc.Bacc("TRN2", target_bir_lowering=False, num_devices=1)
    arrays, args = {}, []
    for name in _INS:
        a = np.ascontiguousarray(laid[name])
        arrays[f"in_{name}"] = a
        args.append(nc.dram_tensor(f"in_{name}", a.shape, mybir.dt.from_np(a.dtype), kind="ExternalInput").ap())
    out = nc.dram_tensor("out_0", laid["x"].shape, F32, kind="ExternalOutput").ap()
    build(nc, *args, out)
    r = run_bass_kernel_spmd(nc, [arrays], core_ids=[0])
    return r.results[0]["out_0"]
```

```python
from contextlib import ExitStack

import concourse.bass as bass
from concourse import mybir

F32 = mybir.dt.float32
BF16 = mybir.dt.bfloat16
I32 = mybir.dt.int32
U32 = mybir.dt.uint32
ALU = mybir.AluOpType
ACT = mybir.ActivationFunctionType
AX = mybir.AxisListType.X

P = 128
EPS = 1e-5
EPS_DEN = 1e-6
RSQRT_MAGIC = float(0x5F3759DF)


def live(index, count):
    return not isinstance(index, int) or 0 <= index < count


def at_least(eng, sem, count):
    if not isinstance(count, int) or count > 0:
        eng.wait_ge(sem, count)


def run_steps(eng, body, first, lo, hi, last, unroll, ring):
    assert (hi - lo) % unroll == 0 and unroll % ring == 0
    for s in range(first, lo):
        body(s, s % ring)
    with eng.Fori(0, (hi - lo) // unroll) as i:
        for s in range(lo, lo + unroll):
            body(i * unroll + s, s % ring)
    for s in range(hi, last):
        body(s, s % ring)


def run_quads(eng, body, first, lo, hi, last):
    assert (hi - lo) % 2 == 0
    for q in range(first, lo):
        for k in range(4):
            body(q, k, q % 2)
    with eng.Fori(0, (hi - lo) // 2) as i:
        for q in range(lo, lo + 2):
            for k in range(4):
                body(i * 2 + q, k, q % 2)
    for q in range(hi, last):
        for k in range(4):
            body(q, k, q % 2)


def tiles(first, count=1):
    return bass.ds(first, count) if not isinstance(first, int) else slice(first, first + count)


def flat(ap):
    return ap.rearrange("p a b -> p (a b)")


class Series:

    def __init__(self, eng, sem, base):
        self.eng, self.sem, self.count = eng, sem, base

    def done(self, ins):
        ins.then_inc(self.sem, 1)
        self.count = self.count + 1

    def wait(self):
        at_least(self.eng, self.sem, self.count)


def rstd_steps(nc, series, st, width, scratch, rs, nm):
    mean_even, sq_even, mean_odd, sq_odd = st[1], st[2], st[4], st[5]
    ve, y, t, mean2 = scratch
    tensor, scalar, fused = nc.vector.tensor_tensor, nc.vector.tensor_scalar, nc.vector.scalar_tensor_tensor
    series.wait()
    yield series.done(tensor(t, mean_even, mean_odd, ALU.subtract))
    yield series.done(tensor(ve, sq_even, sq_odd, ALU.add))
    yield series.done(tensor(mean2, mean_even, mean_odd, ALU.add))
    series.wait()
    yield series.done(scalar(ve, ve, 1.0 / width, EPS, ALU.mult, ALU.add))
    yield series.done(fused(out=t, in0=t, scalar=0.25, in1=t, op0=ALU.mult, op1=ALU.mult))
    series.wait()
    yield series.done(tensor(ve, ve, t, ALU.add))
    series.wait()
    yield series.done(scalar(t.bitcast(I32), ve.bitcast(I32), 1, None, ALU.logical_shift_right))
    series.wait()
    yield series.done(scalar(y.bitcast(I32), t.bitcast(I32), -1.0, RSQRT_MAGIC, ALU.mult, ALU.add))
    for k in range(3):
        series.wait()
        yield series.done(tensor(t, y, y, ALU.mult))
        series.wait()
        yield series.done(fused(out=t, in0=t, scalar=-0.5, in1=ve, op0=ALU.mult, op1=ALU.mult))
        series.wait()
        yield series.done(fused(out=rs if k == 2 else y, in0=t, scalar=1.5, in1=y, op0=ALU.add, op1=ALU.mult))
    series.wait()
    yield fused(out=nm, in0=mean2, scalar=-0.5, in1=rs, op0=ALU.mult, op1=ALU.mult)


RSTD_STEPS = 17
BIAS_AT = 14
NORMS_IN_STEP = (6, 6, 6)
assert sum(NORMS_IN_STEP) == RSTD_STEPS + 1
ALLOC_STEPS = 17


def finish(steps):
    for ins in steps:
        pass
    return ins


def build(nc, x, wq, wk, wv, wo, bq, bk, bv, bo, w_router_t, gate_up, down, w_gate_t, w_up_t, w_down_t, out):
    B, S, D = x.shape
    NH = 16
    HD = D // NH
    E = w_router_t.shape[1]
    F = w_gate_t.shape[1]
    FC = F // P
    NTOK = B * S
    NT = NTOK // P
    TPB = S // P
    ST = (NTOK + E * (P - 1)) // P
    GT = 4
    NG = NT // GT
    QUADS = -(-ST // 4)
    GD = GT * D
    KVW = NH * HD * HD
    CW = D + NH
    assert D == P and TPB == 2 and NT % GT == 0

    RW = 2 * D + 4
    SCALE, SHIFT, TOKEN = 2 * D, 2 * D + 1, 2 * D + 2

    x_dram = x.rearrange("b s d -> (b s) d").rearrange("(t p) d -> p t d", p=P)
    out_rows = out.rearrange("b s d -> (b s) d")
    sorted_rows = nc.dram_tensor("sorted_rows", (ST * P, RW), F32, kind="Internal").ap()
    sorted_tiles = sorted_rows.rearrange("(j p) d -> p j d", p=P)
    cleared_rows = sorted_rows.rearrange("(p j) d -> p j d", p=P)

    with ExitStack() as ctx:
        def sb(name, shape, dt=F32):
            return ctx.enter_context(nc.sbuf_tensor(name, shape, dt))

        def sem(name):
            return ctx.enter_context(nc.semaphore(name))

        col_index = sb("col_index", [P, P])
        row_index = sb("row_index", [P, 1])
        row_start = sb("row_start", [P, 1])
        ident = sb("ident", [P, P])
        upto = sb("upto", [P, P])
        ones = sb("ones", [P, E])
        before_bf = sb("before_bf", [P, P], BF16)
        ones_bf = sb("ones_bf", [P, P], BF16)
        from_last = sb("from_last", [P, E])
        row_index_less = sb("row_index_less", [P, 1])
        head_start = sb("head_start", [P, CW])
        in_head = sb("in_head", [P, CW])
        head_mask = sb("head_mask", [P, CW])
        wait_taker = sb("wait_taker", [P, 1])
        w_qkv = sb("w_qkv", [P, 3 * D])
        w_o = sb("w_o", [P, D])
        w_r = sb("w_r", [P, E])
        w_g = sb("w_g", [P, F])
        w_u = sb("w_u", [P, F])
        w_d = sb("w_d", [P, FC, D])
        w_exp = sb("w_exp", [P, E, 2 * F])
        w_exp_down = sb("w_exp_down", [P, E, FC, D])
        bias = sb("bias", [P, 4 * D])
        bias_left = sb("bias_left", [P, 4 * D])
        bias_part = sb("bias_part", [P, 3, 4 * D], BF16)
        bias_rows = sb("bias_rows", [P, 4 * D], BF16)
        rows = sb("rows", [P, ST, RW])
        stats = sb("stats", [P, NT, 6])
        rs1 = sb("rs1", [P, NT])
        nm1 = sb("nm1", [P, NT])
        scratch1 = sb("scratch1", [P, 4, NT])
        xn = sb("xn", [P, 2, D])
        xnT = sb("xnT", [P, 2, D])
        neg = sb("neg", [P, 2, 2 * D])
        ex = sb("ex", [P, 2, 2 * D])
        rl = sb("rl", [P, 2, 2 * D])
        qk = sb("qk", [P, 4, 2 * D])
        vv = sb("vv", [P, 2, CW])
        qT = sb("qT", [P, D])
        carry = sb("carry", [P, CW])
        carried = sb("carried", [P, CW])
        kv = sb("kv", [P, 4, KVW])
        zq = sb("zq", [P, D])
        den = sb("den", [P, NH])
        rden = sb("rden", [P, NH])
        prod = sb("prod", [P, KVW])
        num = sb("num", [P, D])
        att = sb("att", [P, 2, D])
        attT = sb("attT", [P, D])
        rstd2 = sb("rstd2", [P, 2, GT * (NG + 1)])
        nmean2 = sb("nmean2", [P, 2, GT * (NG + 1)])
        stats2 = sb("stats2", [P, 2, GT, 6])
        scratch2 = sb("scratch2", [P, 4, 2, GT])
        ya = sb("ya", [P, 2, GD])
        xm = sb("xm", [P, 2, GD])
        xmT = sb("xmT", [P, 2, GD])
        silu_g = sb("silu_g", [P, FC, GD])
        hT = sb("hT", [P, FC, GD])
        top = sb("top", [P, 2, GT])
        first_top = sb("first_top", [P, GT])
        is_top = sb("is_top", [P, GT, E])
        chosen = sb("chosen", [P, 2, GT, E], BF16)
        half_tanh = sb("half_tanh", [P, GT])
        score = sb("score", [P, 2, GT])
        taken = sb("taken", [P, 2, E])
        room = sb("room", [P, 2, E])
        shift = sb("shift", [P, 2, E])
        need = sb("need", [P, E], I32)
        given = sb("given", [P, E])
        shift_new = sb("shift_new", [P, E])
        shift_gain = sb("shift_gain", [P, E])
        room_left = sb("room_left", [P, E])
        shift_taken = sb("shift_taken", [P, E])
        moved = sb("moved", [P, E])
        in_new = sb("in_new", [P, GT, E])
        slot_of = sb("slot_of", [P, GT, E])
        slot = sb("slot", [P, GT])
        slot_i = sb("slot_i", [P, NT], I32)
        all_ends = sb("all_ends", [P, NG + 1, E])
        passed = sb("passed", [P, NG, E])
        tile_rank = sb("tile_rank", [P, 1])
        tile_expert = sb("tile_expert", [1, P], I32)
        xs = sb("xs", [P, 2, D])
        xsT = sb("xsT", [P, 2, D])
        w_now = sb("w_now", [P, 2, 2 * F])
        silu_e = sb("silu_e", [P, 2, F])
        hT_e = sb("hT_e", [P, 2, F])
        stats3 = sb("stats3", [P, 4, 6])
        scratch3 = sb("scratch3", [P, 4, 4])
        rstd3 = sb("rstd3", [P, 2, 4])
        nmean3 = sb("nmean3", [P, 2, 4])
        yn = sb("yn", [P, 4, D])
        token_i = sb("token_i", [P, ST], I32)

        pair = [ctx.enter_context(nc.psum_tensor(f"banks{2 * i}", [P, 1024], F32)) for i in range(4)]
        bank = [pair[i // 2][:, 512 * (i % 2):512 * (i % 2 + 1)] for i in range(8)]

        CHUNKS = [(0, 4), (4, 12), (12, NT)]
        s_x = [sem(f"x_loaded{i}") for i in range(len(CHUNKS))]
        s_w = sem("attention_weights_loaded")
        s_bias = sem("bias_loaded")
        s_w2 = sem("ffn_weights_loaded")
        s_wexp = sem("expert_weights_loaded")
        s_iota = sem("indices_written")
        s_const = sem("constants_written")
        s_zero = sem("zeros_written")
        s_cleared = sem("sorted_rows_cleared")
        s_setup = sem("setup_steps")
        s_bias_clear = sem("bias_rows_cleared")
        s_bias_part = sem("bias_parts_made")
        s_bias_left = sem("bias_left_made")
        s_mask_series = sem("mask_steps")
        s_bias_rows = sem("bias_rows_written")
        s_norm1 = sem("norm1_ready")
        s_xn = sem("xn_ready")
        s_xn_t = sem("xn_transposed")
        s_xnT = sem("xnT_ready")
        s_qkv = sem("qkv_projected")
        s_neg = sem("negative_parts_ready")
        s_elu = sem("elu_halves_ready")
        s_v = sem("v_ready")
        s_qk = sem("qk_ready")
        s_kv = sem("kv_ready")
        s_z = sem("z_summed")
        s_q_t = sem("q_transposed")
        s_qT = sem("qT_ready")
        s_carried = sem("carry_multiplied")
        s_c_out = sem("carried_stored")
        s_s = sem("state_summed")
        s_chain = sem("attention_steps")
        s_recip = sem("denominator_inverted")
        s_att = sem("att_ready")
        s_att_t = sem("att_transposed")
        s_attT = sem("attT_ready")
        s_y = sem("y_projected")
        s_y_out = sem("y_stored")

        s_series2 = sem("norm_steps2")
        s_norm2 = sem("norms2_ready")
        s_x1 = sem("residual_added")
        s_ya = sem("attention_normed")
        s_xm = sem("xm_ready")
        s_xm_t = sem("xm_transposed")
        s_xmT = sem("xmT_ready")
        s_gu = sem("shared_gate_up")
        s_silu = sem("shared_silu")
        s_h = sem("shared_h")
        s_sh = sem("shared_down")
        s_sh_out = sem("shared_stored")
        s_logit = sem("logits_ready")
        s_top = sem("top_found")
        s_route = sem("routing_steps")
        s_chosen = sem("expert_chosen")
        s_rank = sem("ranks_counted")
        s_alloc = sem("allocation_steps")
        s_slot = sem("slots_ready")
        s_tanh = sem("half_tanh_ready")
        s_score = sem("score_ready")
        s_scale = sem("scales_ready")
        s_scattered = sem("rows_scattered")
        s_tile_rank = sem("tile_ranks_ready")
        s_tile_row = sem("tile_ranks_turned")
        s_experts = sem("tile_experts_ready")

        s_quad = [sem(f"quad_loaded{i}") for i in range(4)]
        s_loaded = sem("slot_quads_loaded")
        s_xs = sem("xs_ready")
        s_xs_t = sem("xs_transposed")
        s_xsT = sem("xsT_ready")
        s_wn = sem("expert_weights_copied")
        s_gue = sem("expert_gate_up")
        s_silue = sem("expert_silu")
        s_he = sem("expert_h_ready")
        s_de = sem("expert_down")
        s_sum = sem("ffn_summed")
        s_stats3 = sem("ffn_stats_ready")
        s_series3 = sem("norm_steps3")
        s_yn = sem("ffn_normed")
        s_fin = sem("output_ready")
        s_fin_last = sem("last_outputs_ready")
        s_out = sem("output_stored")

        CH = 6
        Z_READ, S_READ = [2, 1], [3, 2]
        SN = RSTD_STEPS + 1
        EXTRA, MAINS_FROM = 2, 12
        SQ = RSTD_STEPS + 1
        NORM_STEPS = [4, 3, 2, 1]
        ADDED_BY_POOL = 4 * (QUADS - 2)

        ps_qkv = [bank[0], bank[1]]
        ps_s = [pair[1], pair[2]]
        ps_xT, ps_o = bank[6], bank[7]
        ps_t2, ps_r, ps_y2, ps_rank = bank[6], bank[0], bank[1], bank[7]
        ps_g, ps_u = [bank[2], bank[3]], [bank[4], bank[5]]
        ps_gue, ps_ye, ps_xs = [bank[2], bank[3]], [bank[0], bank[1]], bank[6]
        ps_turn = bank[5]

        block = ctx.enter_context(nc.Block())

        @block.sync
        def _(sp):
            for c, (t0, t1) in enumerate(CHUNKS):
                sp.dma_start(rows[:, t0:t1, 0:D], x_dram[:, t0:t1, :]).then_inc(s_x[c], 16)
                if c == 0:
                    for n, w in enumerate((wq, wk, wv)):
                        sp.dma_start(w_qkv[:, n * D:(n + 1) * D], w).then_inc(s_w, 16)
                    sp.dma_start(w_o[:], wo).then_inc(s_w, 16)
            sp.dma_start(w_r[:], w_router_t).then_inc(s_w2, 16)
            sp.dma_start(w_g[:], w_gate_t).then_inc(s_w2, 16)
            sp.dma_start(w_u[:], w_up_t).then_inc(s_w2, 16)
            sp.dma_start(w_d[:], w_down_t.rearrange("(c f) h -> f c h", f=P)).then_inc(s_w2, 16)
            sp.wait_ge(s_zero, 1)
            for j in range(0, ST, ST - NT):
                n = min(ST - NT, ST - j)
                sp.dma_start(cleared_rows[:, j:j + n, :], rows[:, NT:NT + n, :]).then_inc(s_cleared, 16)
            for e in range(0, E, 4):
                sp.dma_start(w_exp[:, e:e + 4, :],
                             gate_up[e:e + 4].rearrange("e h f -> h e f")).then_inc(s_wexp, 16)
                for c in range(FC):
                    sp.dma_start(w_exp_down[:, e:e + 4, c, :],
                                 down[e:e + 4, c * P:(c + 1) * P].rearrange("e f h -> f e h")).then_inc(s_wexp, 16)
            sp.wait_ge(s_scattered, 16 * NT)
            quads = [(q, min(q + 4, ST)) for q in range(0, ST, 4)]
            for n, (j0, j1) in enumerate(quads):
                if n >= 4:
                    sp.wait_ge(s_quad[n % 4], 16 * (n // 4))
                    sp.sem_inc(s_loaded, 1)
                sp.dma_start(rows[:, j0:j1, :], sorted_tiles[:, j0:j1, :]).then_inc(s_quad[n % 4], 16)
            for n in range(len(quads), len(quads) + 4):
                sp.wait_ge(s_quad[n % 4], 16 * (n // 4))
                sp.sem_inc(s_loaded, 1)

        @block.gpsimd
        def _(pool):
            whole = dict(allow_small_or_imprecise_dtypes=True)
            nc.gpsimd.iota(col_index[:], [[1, P]], 0, 0, **whole).then_inc(s_iota, 1)
            nc.gpsimd.iota(row_index[:], [[0, 1]], 0, 1, **whole).then_inc(s_iota, 1)
            nc.gpsimd.iota(row_index_less[:], [[0, 1]], 1 - HD, 1, **whole)
            nc.gpsimd.iota(head_start[:, 0:D].rearrange("p (h d) -> p h d", h=NH), [[HD, NH], [0, HD]], 0, 0, **whole)
            nc.gpsimd.iota(head_start[:, D:CW], [[HD, NH]], 0, 0, **whole).then_inc(s_iota, 1)
            nc.gpsimd.iota(row_start[:], [[0, 1]], 0, P, **whole).then_inc(s_iota, 1)
            nc.gpsimd.memset(rows[:, NT:ST, :], 0.0).then_inc(s_zero, 1)
            nc.gpsimd.iota(rows[:, 0:NT, TOKEN], [[-P, NT]], NTOK, -1, **whole)
            nc.gpsimd.memset(rows[:, 0:NT, TOKEN + 1], 0.0)
            nc.gpsimd.memset(bias_rows[:], 0.0).then_inc(s_bias_clear, 1)

            def step1(t, u):
                pool.wait_ge(s_elu, 2 * (t + 1))
                at_least(pool, s_att, t - 3)
                nc.gpsimd.tensor_tensor(qk[:, u, :], ex[:, u % 2, :], rl[:, u % 2, :], ALU.add).then_inc(s_qk, 1)
                pool.wait_ge(s_qk, t + 1)
                pool.wait_ge(s_v, t + 1)
                at_least(pool, s_s, t - 2)
                k = qk[:, u, D:2 * D].rearrange("p (h o d) -> p h o d", h=NH, o=1).to_broadcast([P, NH, HD, HD])
                v = vv[:, u % 2, 0:D].rearrange("p (h m o) -> p h m o", h=NH, o=1).to_broadcast([P, NH, HD, HD])
                nc.gpsimd.tensor_tensor(kv[:, u, :].rearrange("p (h m d) -> p h m d", h=NH, m=HD),
                                        k, v, ALU.mult).then_inc(s_kv, 1)
            run_steps(pool, step1, 0, 4, 28, NT, 8, 4)

            for g in range(NG):
                u = g % 2
                own = slice(GT * g, GT * (g + 1))
                pool.wait_ge(s_tanh, g + 1)
                nc.gpsimd.tensor_scalar(score[:, u, :], half_tanh[:], 0.5, 0.5,
                                        ALU.mult, ALU.add).then_inc(s_score, 1)
                pool.wait_ge(s_score, g + 1)
                pos = slice(GT * (g + 1), GT * (g + 2))
                nc.gpsimd.tensor_tensor(rows[:, own, SCALE], rstd2[:, 0, pos], score[:, u, :],
                                        ALU.mult).then_inc(s_scale, 1)
                nc.gpsimd.tensor_tensor(rows[:, own, SHIFT], nmean2[:, 0, pos], score[:, u, :],
                                        ALU.mult).then_inc(s_scale, 1)
                pool.wait_ge(s_scale, 2 * g + 2)
                pool.wait_ge(s_sh_out, g + 1)
                pool.wait_ge(s_slot, g + 1)
                if g == 0:
                    pool.wait_ge(s_cleared, 16 * len(range(0, ST, ST - NT)))
                for t in range(GT * g, GT * (g + 1)):
                    nc.gpsimd.indirect_dma_start(
                        out=sorted_rows, out_offset=bass.IndirectOffsetOnAxis(ap=slot_i[:, t:t + 1], axis=0),
                        in_=rows[:, t, :], in_offset=None).then_inc(s_scattered, 16)

            for j in range(ST + 1):
                if j < ADDED_BY_POOL:
                    r = flat(rows[:, j:j + 1, 0:D])
                    pool.wait_ge(s_yn, j + 1)
                    nc.gpsimd.tensor_tensor(r, r, yn[:, j % 4, :], ALU.add).then_inc(s_fin, 1)
                if j > 0:
                    if j <= ADDED_BY_POOL:
                        pool.wait_ge(s_fin, j)
                    else:
                        pool.wait_ge(s_fin_last, j - ADDED_BY_POOL)
                    nc.gpsimd.indirect_dma_start(
                        out=out_rows, out_offset=bass.IndirectOffsetOnAxis(ap=token_i[:, j - 1:j], axis=0),
                        in_=rows[:, j - 1, 0:D], in_offset=None,
                        bounds_check=NTOK - 1, oob_is_err=False).then_inc(s_out, 16)
            pool.wait_ge(s_out, 16 * ST)

        @block.scalar
        def _(act):
            for n, b in enumerate((bq, bk, bv, bo)):
                act.dma_start(bias[:, n * D:(n + 1) * D],
                               b.rearrange("(o d) -> o d", o=1).to_broadcast([P, D])).then_inc(s_bias, 16)

            def bias_row(n):
                if n:
                    act.wait_ge(s_bias_left, n)
                nc.scalar.copy(bias_part[:, n, :], (bias_left if n else bias)[:]).then_inc(s_bias_part, 1)
                act.wait_ge(s_bias_part, n + 1)
                row = slice(32 * n, 32 * n + 1)
                nc.scalar.copy(bias_rows[row, :], bias_part[row, n, :]).then_inc(s_bias_rows, 1)

            act.wait_ge(s_bias, 64)
            act.wait_ge(s_bias_clear, 1)
            bias_row(0)
            bias_row(1)

            def step1(t, u):
                if live(t + 4, NT):
                    at = t + 4
                    act.wait_ge(s_norm1, len(CHUNKS) if not isinstance(t, int) else
                                1 + max(c for c, (t0, _) in enumerate(CHUNKS) if t0 <= at))
                    at_least(act, s_xn_t, t + 3)
                    nc.scalar.activation(xn[:, u % 2, :], flat(rows[:, tiles(at), 0:D]), ACT.Identity,
                                         bias=nm1[:, tiles(at)], scale=rs1[:, tiles(at)]).then_inc(s_xn, 1)
                if live(t + 3, NT):
                    act.wait_ge(s_xn_t, t + 4)
                    at_least(act, s_qkv, t + 2)
                    if u % 2 and live(t, NT):
                        act.wait_ge(s_q_t, t + 1)
                    nc.scalar.copy(xnT[:, (u + 3) % 2, :], ps_xT[:, 0:D]).then_inc(s_xnT, 1)
                if isinstance(t, int) and t == -3:
                    bias_row(2)
                if u % 2 and live(t, NT):
                    act.wait_ge(s_q_t, t + 1)
                    at_least(act, s_carried, t - 1)
                    nc.scalar.copy(qT[:], ps_xT[:, D:2 * D]).then_inc(s_qT, 2)
                if live(t - 2, NT):
                    act.wait_ge(s_att_t, t - 1)
                    at_least(act, s_y, t - 2)
                    nc.scalar.copy(attT[:], ps_o[:, 0:D]).then_inc(s_attT, 1)
                if live(t + 2, NT):
                    act.wait_ge(s_qkv, t + 3)
                    at_least(act, s_qk, t + 1)
                    nc.scalar.activation(neg[:, u % 2, :], ps_qkv[u % 2][:, 0:2 * D], ACT.Relu, scale=-1.0).then_inc(s_neg, 1)
                    nc.scalar.activation(rl[:, u % 2, :], ps_qkv[u % 2][:, 0:2 * D], ACT.Relu).then_inc(s_elu, 1)
                    act.wait_ge(s_neg, t + 3)
                    nc.scalar.activation(ex[:, u % 2, :], neg[:, u % 2, :], ACT.Exp, scale=-1.0).then_inc(s_elu, 1)
                    at_least(act, s_kv, t + 1)
                    nc.scalar.copy(vv[:, u % 2, 0:D], ps_qkv[u % 2][:, 2 * D:3 * D]).then_inc(s_v, 1)
                if live(t - 2, NT):
                    act.wait_ge(s_y, t - 1)
                    nc.scalar.copy(flat(rows[:, tiles(t - 2), D:2 * D]), ps_o[:, D:2 * D]).then_inc(s_y_out, 1)
                if u % 2 and live(t, NT):
                    act.wait_ge(s_carried, t + 1)
                    at_least(act, s_att, t - 1)
                    nc.scalar.copy(carried[:], ps_xT[:, 2 * D:2 * D + CW]).then_inc(s_c_out, 2)

            def step2(s, u):
                if live(s, NG):
                    for f in range(FC):
                        act.wait_ge(s_gu, 2 * s + 1 + f)
                        at_least(act, s_h, 2 * s - 1 + f)
                        nc.scalar.activation(silu_g[:, f, :], ps_g[f][:], ACT.Silu).then_inc(s_silu, 1)
                if live(s + 1, NG):
                    act.wait_ge(s_xm_t, s + 2)
                    at_least(act, s_logit, s)
                    nc.scalar.copy(xmT[:, (u + 1) % 2, :], ps_t2[:]).then_inc(s_xmT, 1)
                if live(s + 3, NG):
                    act.wait_ge(s_norm2, s + 4)
                    for k in range(GT):
                        c = tiles(GT * (s + 3) + k)
                        ins = nc.scalar.activation(
                            ya[:, (u + 1) % 2, k * D:(k + 1) * D], flat(rows[:, c, D:2 * D]),
                            ACT.Identity, bias=nmean2[:, 1, c], scale=rstd2[:, 1, c])
                        if k % 2:
                            ins.then_inc(s_ya, 1)
                if live(s + 2, NG):
                    act.wait_ge(s_norm2, s + 4)
                    at_least(act, s_xm_t, s + 1)
                    for k in range(GT):
                        c = tiles(GT * (s + 3) + k)
                        ins = nc.scalar.activation(
                            xm[:, u % 2, k * D:(k + 1) * D], flat(rows[:, tiles(GT * (s + 2) + k), 0:D]),
                            ACT.Identity, bias=nmean2[:, 0, c], scale=rstd2[:, 0, c])
                    ins.then_inc(s_xm, 1)
                if live(s, NG):
                    act.wait_ge(s_top, s + 1)
                    at_least(act, s_score, s)
                    nc.scalar.activation(half_tanh[:], top[:, u, :], ACT.Tanh, scale=0.5).then_inc(s_tanh, 1)
                    act.wait_ge(s_sh, s + 1)
                    nc.scalar.copy(rows[:, tiles(GT * s, GT), D:2 * D],
                                   ps_y2[:].rearrange("p (t d) -> p t d", d=D)).then_inc(s_sh_out, 1)

            run_steps(act, step1, -4, 4, 28, NT - 2, 8, 4)
            step2(-3, 1)
            step1(NT - 2, 2)
            step1(NT - 1, 3)
            step2(-2, 0)
            step1(NT, 0)
            step1(NT + 1, 1)
            run_steps(act, step2, -1, 1, 5, NG, 2, 2)

            act.wait_ge(s_experts, 1)
            act.wait_ge(s_wexp, 16 * (E // 4) * (1 + FC))

            def step3(q, u, parity):
                j = 4 * q + u
                if live(j + 4, ST):
                    e = act.value_load(tile_expert[0:1, tiles(j + 4)], min_val=0, max_val=E - 1)
                    if u == 0:
                        act.wait_ge(s_loaded, q + 2)
                    at_least(act, s_xs_t, j + 3)
                    r = rows[:, tiles(j + 4), :]
                    nc.scalar.activation(xs[:, u % 2, :], flat(r[:, :, 0:D]), ACT.Identity,
                                         bias=flat(r[:, :, SHIFT:SHIFT + 1]),
                                         scale=flat(r[:, :, SCALE:SCALE + 1])).then_inc(s_xs, 1)
                if live(j + 3, ST):
                    act.wait_ge(s_xs_t, j + 4)
                    at_least(act, s_gue, j + 2)
                    nc.scalar.copy(xsT[:, (u + 1) % 2, :], ps_xs[:, 0:D]).then_inc(s_xsT, 1)
                if live(j + 2, ST):
                    act.wait_ge(s_gue, j + 3)
                    at_least(act, s_he, j + 1)
                    nc.scalar.activation(silu_e[:, u % 2, :], ps_gue[u % 2][:, 0:F], ACT.Silu).then_inc(s_silue, 1)
                if live(j + 4, ST):
                    nc.scalar.copy(w_now[:, u % 2, :], flat(w_exp[:, bass.ds(e, 1), :])).then_inc(s_wn, 1)
            run_quads(act, step3, -1, 1, 9, 12)

        @block.vector
        def _(dve):
            setup = Series(dve, s_setup, 0)
            dve.wait_ge(s_iota, 2)
            nc.vector.tensor_scalar(ident[:], col_index[:], row_index[:], None, ALU.is_equal).then_inc(s_const, 1)

            def stats_of(t0, t1):
                for t in range(t0, t1):
                    yield nc.vector.bn_stats(stats[:, t, :], rows[:, t, 0:D])

            def norm_chunk(c, series):
                r = slice(*CHUNKS[c])
                return rstd_steps(nc, series, [stats[:, r, n] for n in range(6)], D,
                                  [scratch1[:, n, r] for n in range(4)], rs1[:, r], nm1[:, r])

            def constant_steps(series):
                yield nc.vector.memset(ones_bf[:], 1.0).then_inc(s_const, 1)
                yield nc.vector.tensor_scalar(upto[:], col_index[:], row_index[:], None, ALU.is_ge).then_inc(s_const, 1)
                yield nc.vector.memset(vv[:, :, D:CW], 1.0).then_inc(s_const, 1)
                yield nc.vector.tensor_scalar(before_bf[:], col_index[:], row_index[:], None,
                                              ALU.is_gt).then_inc(s_const, 1)
                yield nc.vector.tensor_scalar(from_last[:], col_index[:, 0:E], -1.0, float(E),
                                              ALU.mult, ALU.add).then_inc(s_const, 1)
                yield nc.vector.memset(ones[:, 0:E], 1.0)
                dve.wait_ge(s_iota, 3)
                yield nc.vector.tensor_scalar(in_head[:], head_start[:], row_index_less[:], None, ALU.is_ge)
                yield series.done(nc.vector.tensor_scalar(head_mask[:], head_start[:], row_index[:], None, ALU.is_le))
                series.wait()
                yield series.done(nc.vector.tensor_tensor(head_mask[:], head_mask[:], in_head[:], ALU.mult))
                yield nc.vector.memset(taken[:, 1, :], 0.0)
                yield nc.vector.memset(room[:, 1, :], 0.0)
                yield nc.vector.memset(shift[:, 1, :], 0.0)
                yield nc.vector.memset(all_ends[:, 0, :], 0.0).then_inc(s_const, 1)

            dve.wait_ge(s_x[0], 16)
            setup.done(finish(stats_of(*CHUNKS[0])))
            constants = constant_steps(Series(dve, s_mask_series, 0))

            def left_of_bias(n):
                dve.wait_ge(s_bias_part, n + 1)
                if n:
                    dve.wait_ge(s_bias_left, n)
                nc.vector.tensor_tensor(bias_left[:], (bias_left if n else bias)[:], bias_part[:, n, :],
                                        ALU.subtract).then_inc(s_bias_left, 1)

            for n, ins in enumerate(norm_chunk(0, setup)):
                last = ins
                if n % 2:
                    next(constants)
                if n == BIAS_AT:
                    left_of_bias(0)
            last.then_inc(s_norm1, 1)
            left_of_bias(1)
            dve.wait_ge(s_x[1], 16)
            setup.done(finish(stats_of(*CHUNKS[1])))
            later = stats_of(*CHUNKS[2])
            dve.wait_ge(s_x[2], 16)
            for ins in norm_chunk(1, setup):
                last = ins
                next(constants, None), next(later)
            last.then_inc(s_norm1, 1)
            setup.done(finish(later))
            last_norms = norm_chunk(2, setup)

            def first_step1(t, u):
                if isinstance(t, int) and t <= 2:
                    step1(t, u, norms_of_last_chunk(t), 1)
                else:
                    step1(t, u)

            def norms_of_last_chunk(t):
                for n in range(NORMS_IN_STEP[t]):
                    ins = next(last_norms)
                    if t == 2 and n == NORMS_IN_STEP[t] - 1:
                        ins.then_inc(s_norm1, 1)
                    yield ins

            def step1(t, u, others=iter(()), between=3):
                def other(count=between):
                    for _ in range(count):
                        next(others, None)
                multiplied = S_READ[u % 2]
                if live(t, NT):
                    dve.wait_ge(s_z, t + 1)
                    nc.vector.tensor_tensor(zq[:], ps_qkv[u % 2][:, 3 * D:4 * D], qk[:, u, 0:D],
                                            ALU.mult).then_inc(s_chain, 1)
                    other()
                if u % 2 == 0 and live(t, NT):
                    nc.vector.tensor_tensor(carry[:], ps_qkv[0][:, 0:CW], head_mask[:], ALU.mult).then_inc(s_chain, 1)
                    other()
                if live(t - 1, NT):
                    dve.wait_ge(s_chain, CH * (t - 1) + S_READ[1 - u % 2] + 3)
                    nc.vector.reciprocal(rden[:], rden[:]).then_inc(s_recip, 1)
                    other()
                if live(t, NT):
                    dve.wait_ge(s_s, t + 1)
                    nc.vector.tensor_tensor(
                        prod[:].rearrange("p (h m d) -> p h m d", h=NH, m=HD),
                        ps_s[u % 2][:].rearrange("p (h m d) -> p h m d", h=NH, m=HD),
                        qk[:, u, 0:D].rearrange("p (h o d) -> p h o d", h=NH, o=1).to_broadcast([P, NH, HD, HD]),
                        ALU.mult).then_inc(s_chain, 1)
                    other()
                if live(t - 1, NT):
                    dve.wait_ge(s_recip, t)
                    dve.wait_ge(s_chain, CH * t)
                    at_least(dve, s_att_t, t - 2)
                    nc.vector.tensor_tensor(att[:, 1 - u % 2, :].rearrange("p (h m) -> p h m", h=NH),
                                            num[:].rearrange("p (h m) -> p h m", h=NH),
                                            rden[:].rearrange("p (h o) -> p h o", o=1).to_broadcast([P, NH, HD]),
                                            ALU.mult).then_inc(s_att, 1)
                    other()
                if live(t, NT):
                    dve.wait_ge(s_chain, CH * t + Z_READ[u % 2])
                    nc.vector.tensor_reduce(den[:], zq[:].rearrange("p (h d) -> p h d", h=NH), AX,
                                            ALU.add).then_inc(s_chain, 1)
                    other()
                    dve.wait_ge(s_chain, CH * t + multiplied)
                    at_least(dve, s_att, t)
                    nc.vector.tensor_reduce(num[:], prod[:].rearrange("p (n d) -> p n d", d=HD), AX,
                                            ALU.add).then_inc(s_chain, 1)
                    other()
                    dve.wait_ge(s_chain, CH * t + multiplied + 1)
                    if u % 2 == 0:
                        nc.vector.tensor_scalar(rden[:], den[:], EPS_DEN, None, ALU.add).then_inc(s_chain, 1)
                        other()
                    else:
                        dve.wait_ge(s_c_out, t + 1)
                        nc.vector.scalar_tensor_tensor(out=rden[:], in0=den[:], scalar=EPS_DEN, in1=carried[:, D:CW],
                                                       op0=ALU.add, op1=ALU.add).then_inc(s_chain, 1)
                        other()
                        dve.wait_ge(s_chain, CH * t + multiplied + 2)
                        nc.vector.tensor_tensor(num[:], num[:], carried[:, 0:D], ALU.add).then_inc(s_chain, 1)
                        other()
                other(99)

            def slot_steps(g, u):
                dve.wait_ge(s_rank, g + 1)
                last, now = 1 - u, u
                sr = Series(dve, s_alloc, ALLOC_STEPS * g)
                tensor, scalar, fused = nc.vector.tensor_tensor, nc.vector.tensor_scalar, nc.vector.scalar_tensor_tensor

                def wide(ap):
                    return ap.rearrange("p (o e) -> p o e", o=1).to_broadcast([P, GT, E])
                ranks = ps_rank[:, 0:GT * E].rearrange("p (t e) -> p t e", e=E)
                totals = ps_rank[:, GT * E:(GT + 1) * E]
                yield sr.done(tensor(taken[:, now, :], taken[:, last, :], totals, ALU.add))
                yield sr.done(tensor(room_left[:], room[:, last, :], taken[:, last, :], ALU.subtract))
                yield sr.done(tensor(shift_taken[:], shift[:, last, :], taken[:, last, :], ALU.add))
                sr.wait()
                yield sr.done(fused(out=need[:], in0=taken[:, now, :], scalar=float(P - 1), in1=room[:, last, :],
                                    op0=ALU.add, op1=ALU.subtract))
                yield sr.done(tensor(in_new[:], ranks, wide(room_left[:]), ALU.is_ge))
                yield sr.done(tensor(slot_of[:], ranks, wide(shift_taken[:]), ALU.add))
                sr.wait()
                yield sr.done(scalar(need[:], need[:], 7, 7, ALU.logical_shift_right, ALU.logical_shift_left))
                sr.wait()
                yield sr.done(nc.vector.tensor_tensor_scan(given[:], ones[:, 0:E], need[:], 0.0, ALU.mult, ALU.add))
                yield sr.done(tensor(room[:, now, :], room[:, last, :], need[:], ALU.add))
                sr.wait()
                ends = flat(all_ends[:, tiles(g + 1), :])
                yield sr.done(scalar(ends, given[:], flat(all_ends[:, tiles(g), E - 1:E]), None, ALU.add))
                sr.wait()
                yield sr.done(tensor(shift_new[:], ends, room[:, now, :], ALU.subtract))
                sr.wait()
                yield sr.done(tensor(shift_gain[:], shift_new[:], shift[:, last, :], ALU.subtract))
                sr.wait()
                yield sr.done(tensor(in_new[:], in_new[:], wide(shift_gain[:]), ALU.mult))
                yield sr.done(fused(out=moved[:], in0=need[:], scalar=0.0, in1=shift_gain[:],
                                    op0=ALU.is_gt, op1=ALU.mult))
                sr.wait()
                yield sr.done(tensor(slot_of[:], slot_of[:], in_new[:], ALU.add))
                yield tensor(shift[:, now, :], shift[:, last, :], moved[:], ALU.add)
                sr.wait()
                yield sr.done(tensor(slot_of[:], slot_of[:], chosen[:, now, :, :], ALU.mult))
                sr.wait()
                yield sr.done(nc.vector.tensor_reduce(slot[:], slot_of[:], AX, ALU.add))
                sr.wait()
                yield nc.vector.tensor_copy(slot_i[:, tiles(GT * g, GT)], slot[:]).then_inc(s_slot, 1)

            def h_and_choice_steps(s, u):
                logits = ps_r[:, 0:GT * E].rearrange("p (k e) -> p k e", e=E)

                def h(f):
                    dve.wait_ge(s_silu, 2 * s + 1 + f)
                    at_least(dve, s_sh, s)
                    return nc.vector.tensor_tensor(hT[:, f, :], silu_g[:, f, :], ps_u[f][:], ALU.mult).then_inc(s_h, 1)
                final = isinstance(s, int) and s == NG - 1
                if not final:
                    yield h(0)
                dve.wait_ge(s_logit, s + 1)
                yield nc.vector.tensor_reduce(top[:, u, :], logits, AX, ALU.max).then_inc(s_top, 1)
                if not final:
                    yield h(1)
                dve.wait_ge(s_top, s + 1)
                yield nc.vector.tensor_tensor(
                    is_top[:], logits, top[:, u, :].rearrange("p (k o) -> p k o", o=1).to_broadcast([P, GT, E]),
                    ALU.is_equal).then_inc(s_route, 1)
                dve.wait_ge(s_route, 3 * s + 1)
                yield nc.vector.tensor_tensor(
                    is_top[:], is_top[:], from_last[:].rearrange("p (o e) -> p o e", o=1).to_broadcast([P, GT, E]),
                    ALU.mult).then_inc(s_route, 1)
                dve.wait_ge(s_route, 3 * s + 2)
                yield nc.vector.tensor_reduce(first_top[:], is_top[:], AX, ALU.max).then_inc(s_route, 1)
                dve.wait_ge(s_route, 3 * s + 3)
                yield nc.vector.tensor_tensor(
                    chosen[:, u, :, :], is_top[:],
                    first_top[:].rearrange("p (k o) -> p k o", o=1).to_broadcast([P, GT, E]),
                    ALU.is_equal).then_inc(s_chosen, 1)
                if final:
                    yield h(0)
                    yield h(1)

            def prepare_steps(s, u):
                norm = Series(dve, s_series2, SN * (s + 3))
                if isinstance(s, int) and s <= 0:
                    dve.wait_ge(s_y_out, NT if s == 0 else GT * (s + 4))
                if live(s + 3, NG):
                    for k in range(GT):
                        ins = nc.vector.bn_stats(stats2[:, 1, k, :], flat(rows[:, tiles(GT * (s + 3) + k), D:2 * D]))
                        if k < GT - 1 or live(s + 2, NG):
                            yield ins
                if live(s + 2, NG):
                    for half in range(2):
                        dve.wait_ge(s_ya, 2 * (s + 2) + 1 + half)
                        xg = rows[:, tiles(GT * (s + 2) + 2 * half, 2), 0:D]
                        yield nc.vector.tensor_tensor(
                            xg, xg, ya[:, u % 2, 2 * half * D:2 * (half + 1) * D].rearrange("p (t d) -> p t d", d=D),
                            ALU.add).then_inc(s_x1, 1)
                    dve.wait_ge(s_x1, 2 * (s + 3))
                    nc.vector.memset(wait_taker[:], 0.0)
                    for k in range(GT):
                        ins = nc.vector.bn_stats(stats2[:, 0, k, :], flat(rows[:, tiles(GT * (s + 2) + k), 0:D]))
                        if k < GT - 1:
                            yield ins
                kinds = slice(0 if live(s + 2, NG) else 1, 2 if live(s + 3, NG) else 1)
                if kinds.start < kinds.stop:
                    norm.done(ins)
                    yield ins
                    c = tiles(GT * (s + 3), GT)
                    steps = rstd_steps(nc, norm, [stats2[:, kinds, :, n] for n in range(6)], D,
                                       [scratch2[:, n, kinds, :] for n in range(4)],
                                       rstd2[:, kinds, c], nmean2[:, kinds, c])
                    for n, ins in enumerate(steps):
                        if n == RSTD_STEPS:
                            ins.then_inc(s_norm2, 1)
                        yield ins

            def step2(s, u):
                slots = slot_steps(s - 1, 1 - u) if live(s - 1, NG) else iter(())
                mains = h_and_choice_steps(s, u) if live(s, NG) else iter(())
                for n, ins in enumerate(prepare_steps(s, u)):
                    for _ in range(EXTRA if n == GT - 1 else 1):
                        next(slots, None)
                    if n >= MAINS_FROM and (n - MAINS_FROM) % 2 == 0:
                        next(mains, None)
                for ins in slots:
                    pass
                for ins in mains:
                    pass

            run_steps(dve, first_step1, 0, 4, 28, 28, 8, 4)
            step1(NT - 4, 0, prepare_steps(-3, 1))
            step1(NT - 3, 1)
            step1(NT - 2, 2, prepare_steps(-2, 0))
            step1(NT - 1, 3)
            step1(NT, 0)
            run_steps(dve, step2, -1, 1, 5, NG + 1, 2, 2)

            dve.wait_ge(s_slot, NG)
            dve.wait_ge(s_iota, 4)
            setup.done(nc.vector.tensor_scalar(flat(passed[:]), flat(all_ends[:, 1:, :]), row_start[:], None, ALU.is_le))
            setup.wait()
            nc.vector.tensor_reduce(tile_rank[:], flat(passed[:]), AX, ALU.add).then_inc(s_tile_rank, 1)
            dve.wait_ge(s_tile_row, 1)
            setup.done(nc.vector.tensor_copy(tile_expert[:], ps_turn[0:1, 0:P]))
            setup.wait()
            nc.vector.tensor_scalar(tile_expert[:], tile_expert[:], E - 1, None, ALU.bitwise_and).then_inc(s_experts, 1)

            norms3 = {}

            def step3(q, u, parity):
                j = 4 * q + u

                def norm_step(count=1):
                    for _ in range(count):
                        next(norms3["steps"], None)

                if u == 0 and live(q - 1, QUADS):
                    n = min(4, ST - 4 * (q - 1)) if isinstance(q, int) else 4
                    norm = Series(dve, s_series3, SQ * (q - 1))
                    norms3["n"] = n
                    norms3["steps"] = norm_quad(q, n, norm, 1 - parity)
                elif u == 0:
                    norms3["steps"] = iter(())
                if live(j - 8, ST):
                    i = tiles(j - 8)
                    if u == 0:
                        dve.wait_ge(s_series3, SQ * (q - 1))
                    if live(j - 12, ST):
                        dve.wait_ge(s_fin, min(j - 11, ADDED_BY_POOL) if isinstance(j, int) else j - 11)
                    nc.vector.tensor_scalar(yn[:, u, :], flat(rows[:, i, D:2 * D]), rstd3[:, parity, u:u + 1],
                                            nmean3[:, parity, u:u + 1], ALU.mult, ALU.add).then_inc(s_yn, 1)
                if u:
                    norm_step()
                at_least(dve, s_sum, min(j, ST) if isinstance(j, int) else j)
                if live(j + 2, ST):
                    dve.wait_ge(s_silue, j + 3)
                    at_least(dve, s_de, j + 1)
                    nc.vector.tensor_tensor(hT_e[:, u % 2, :], silu_e[:, u % 2, :], ps_gue[u % 2][:, F:2 * F],
                                            ALU.mult).then_inc(s_he, 1)
                if u:
                    norm_step()
                if live(j - 1, ST):
                    nc.vector.bn_stats(stats3[:, (u + 3) % 4, :],
                                       flat(rows[:, tiles(j - 1), D:2 * D])).then_inc(s_stats3, 1)
                norm_step()
                if live(j - 8, ST) and isinstance(j, int) and j - 8 >= ADDED_BY_POOL:
                    dve.wait_ge(s_yn, j - 7)
                    nc.vector.tensor_tensor(flat(rows[:, i, 0:D]), flat(rows[:, i, 0:D]), yn[:, u, :],
                                            ALU.add).then_inc(s_fin_last, 1)
                if live(j, ST):
                    r = flat(rows[:, tiles(j), D:2 * D])
                    dve.wait_ge(s_de, j + 1)
                    nc.vector.tensor_tensor(r, ps_ye[u % 2][:, 0:D], r, ALU.add).then_inc(s_sum, 1)
                norm_step(NORM_STEPS[u])
                if u == 3:
                    norm_step(20)

            def norm_quad(q, n, norm, parity):
                dve.wait_ge(s_stats3, min(4 * q, ST) if isinstance(q, int) else 4 * q)
                for ins in rstd_steps(nc, norm, [stats3[:, 0:n, k] for k in range(6)], D,
                                      [scratch3[:, k, 0:n] for k in range(4)], rstd3[:, parity, 0:n],
                                      nmean3[:, parity, 0:n]):
                    last = ins
                    yield ins
                norm.done(last)
                c = tiles(4 * (q - 1), n)
                yield nc.vector.tensor_scalar(token_i[:, c], rows[:, c, TOKEN], -1.0, float(NTOK),
                                              ALU.mult, ALU.add)

            run_quads(dve, step3, -1, 3, 11, QUADS + 2)

        @block.tensor
        def _(pe):
            def step1(t, u):
                odd = u % 2
                if live(t, NT):
                    pe.wait_ge(s_qk, t + 1)
                    pe.wait_ge(s_v, t + 1)
                    if isinstance(t, int) and t == 0:
                        pe.wait_ge(s_const, 4)
                    ins = nc.tensor.matmul(ps_qkv[u % 2][:, 3 * D:4 * D], upto[:], qk[:, u, D:2 * D],
                                           start=True, stop=True)
                    if not odd:
                        ins = nc.tensor.matmul(ps_qkv[0][:, 0:CW], qk[:, u, D:2 * D], vv[:, 0, :],
                                               start=True, stop=True)
                    ins.then_inc(s_z, 1)
                    pe.wait_ge(s_kv, t + 1)
                    at_least(pe, s_chain, CH * (t - 2) + S_READ[odd])
                    for half in range(2):
                        cols = slice(half * 512, (half + 1) * 512)
                        ins = nc.tensor.matmul(ps_s[u % 2][:, cols], upto[:], kv[:, u, cols], start=True, stop=True)
                    ins.then_inc(s_s, 1)
                if not odd and live(t - 1, NT):
                    pe.wait_ge(s_c_out, t)
                if live(t + 3, NT):
                    pe.wait_ge(s_xn, t + 4)
                    at_least(pe, s_xnT, t + 3)
                    nc.tensor.transpose(ps_xT[:, 0:D], xn[:, (u + 3) % 2, :], ident[:]).then_inc(s_xn_t, 1)
                if odd and live(t, NT):
                    nc.tensor.transpose(ps_xT[:, D:2 * D], qk[:, u, 0:D], ident[:]).then_inc(s_q_t, 2)
                if live(t - 2, NT):
                    pe.wait_ge(s_att, t - 1)
                    at_least(pe, s_y_out, t - 2)
                    nc.tensor.transpose(ps_o[:, 0:D], att[:, u % 2, :], ident[:]).then_inc(s_att_t, 1)
                if live(t + 2, NT):
                    pe.wait_ge(s_xnT, t + 3)
                    if isinstance(t, int) and t == -2:
                        pe.wait_ge(s_const, 2)
                        pe.wait_ge(s_bias_rows, 3)
                        pe.wait_ge(s_w, 64)
                    at_least(pe, s_chain, CH * t + Z_READ[odd])
                    nc.tensor.matmul(ps_qkv[u % 2][:, 0:3 * D], ones_bf[:], bias_rows[:, 0:3 * D],
                                     start=True, stop=False)
                    nc.tensor.matmul(ps_qkv[u % 2][:, 0:3 * D], xnT[:, u % 2, :], w_qkv[:],
                                     start=False, stop=True).then_inc(s_qkv, 1)
                if live(t - 2, NT):
                    pe.wait_ge(s_attT, t - 1)
                    nc.tensor.matmul(ps_o[:, D:2 * D], ones_bf[:], bias_rows[:, 3 * D:4 * D],
                                     start=True, stop=False)
                    nc.tensor.matmul(ps_o[:, D:2 * D], attT[:], w_o[:], start=False, stop=True).then_inc(s_y, 1)
                if odd and live(t, NT):
                    pe.wait_ge(s_qT, t + 1)
                    pe.wait_ge(s_chain, CH * (t - 1) + Z_READ[0])
                    nc.tensor.matmul(ps_xT[:, 2 * D:2 * D + CW], qT[:], carry[:], start=True, stop=True
                                     ).then_inc(s_carried, 2)
            pe.wait_ge(s_const, 1)
            run_steps(pe, step1, -3, 4, 28, NT + 2, 8, 4)

            def step2(s, u):
                def gate_up_of(f):
                    if live(s, NG):
                        at_least(pe, s_h, 2 * s - 1 + f)
                        nc.tensor.matmul(ps_g[f][:], w_g[:, f * P:(f + 1) * P], xmT[:, u % 2, :],
                                         start=True, stop=True)
                        nc.tensor.matmul(ps_u[f][:], w_u[:, f * P:(f + 1) * P], xmT[:, u % 2, :],
                                         start=True, stop=True).then_inc(s_gu, 1)

                if live(s, NG):
                    pe.wait_ge(s_xmT, s + 1)
                gate_up_of(0)
                if live(s, NG):
                    at_least(pe, s_chosen, s)
                    for k in range(GT):
                        ins = nc.tensor.matmul(ps_r[:, k * E:(k + 1) * E], xmT[:, u % 2, k * P:(k + 1) * P],
                                               w_r[:], start=True, stop=True)
                    ins.then_inc(s_logit, 1)
                gate_up_of(1)
                if live(s + 1, NG):
                    pe.wait_ge(s_xm, s + 2)
                    at_least(pe, s_xmT, s + 1)
                    for k in range(GT):
                        ins = nc.tensor.transpose(ps_t2[:, k * P:(k + 1) * P],
                                                  xm[:, (u + 1) % 2, k * D:(k + 1) * D], ident[:])
                    ins.then_inc(s_xm_t, 1)
                def rank():
                    n = GT * E
                    pick = chosen[:, u, :, :].rearrange("p k e -> p (k e)")
                    pe.wait_ge(s_chosen, s + 1)
                    nc.tensor.matmul(ps_rank[:, 0:n], before_bf[:], pick, start=True, stop=False)
                    for k in range(1, GT):
                        nc.tensor.matmul(ps_rank[:, k * E:n], ones_bf[:], pick[:, 0:n - k * E],
                                         start=False, stop=k == GT - 1)
                    for k in range(GT):
                        ins = nc.tensor.matmul(ps_rank[:, n:n + E], ones_bf[:], pick[:, k * E:(k + 1) * E],
                                               start=k == 0, stop=k == GT - 1)
                    ins.then_inc(s_rank, 1)
                if isinstance(s, int) and s == NG - 1:
                    rank()
                if live(s, NG):
                    pe.wait_ge(s_h, 2 * s + 2)
                    at_least(pe, s_sh_out, s)
                    for k in range(GT):
                        for f in range(FC):
                            ins = nc.tensor.matmul(ps_y2[:, k * D:(k + 1) * D], hT[:, f, k * P:(k + 1) * P],
                                                   w_d[:, f, :], start=f == 0, stop=f == FC - 1)
                    ins.then_inc(s_sh, 1)
                if live(s, NG) and not (isinstance(s, int) and s == NG - 1):
                    rank()

            pe.wait_ge(s_w2, 64)
            pe.wait_ge(s_const, 7)
            pe.wait_ge(s_xnT, NT)
            pe.wait_ge(s_c_out, NT)
            step2(-1, 1)
            pe.wait_ge(s_chain, CH * NT)
            pe.wait_ge(s_y_out, NT)
            run_steps(pe, step2, 0, 1, 7, NG, 2, 2)

            pe.wait_ge(s_tile_rank, 1)
            nc.tensor.matmul(ps_turn[0:1, 0:P], tile_rank[:], ident[:], start=True, stop=True).then_inc(s_tile_row, 1)

            def step3(q, u, parity):
                j = 4 * q + u
                if live(j, ST):
                    e = pe.value_load(tile_expert[0:1, tiles(j)], min_val=0, max_val=E - 1)
                if live(j + 3, ST):
                    pe.wait_ge(s_xs, j + 4)
                    at_least(pe, s_xsT, j + 3)
                    nc.tensor.transpose(ps_xs[:, 0:D], xs[:, (u + 1) % 2, :], ident[:]).then_inc(s_xs_t, 1)
                if live(j + 2, ST):
                    pe.wait_ge(s_xsT, j + 3)
                    pe.wait_ge(s_wn, j + 3)
                    at_least(pe, s_he, j + 1)
                    for c in range(2 * FC):
                        ins = nc.tensor.matmul(ps_gue[u % 2][:, c * P:(c + 1) * P],
                                               w_now[:, u % 2, c * P:(c + 1) * P], xsT[:, u % 2, :],
                                               start=True, stop=True)
                    ins.then_inc(s_gue, 1)
                if live(j, ST):
                    pe.wait_ge(s_he, j + 1)
                    at_least(pe, s_sum, j - 1)
                    for c in range(FC):
                        ins = nc.tensor.matmul(ps_ye[u % 2][:, 0:D], hT_e[:, u % 2, c * P:(c + 1) * P],
                                               flat(w_exp_down[:, bass.ds(e, 1), c, :]),
                                               start=c == 0, stop=c == FC - 1)
                    ins.then_inc(s_de, 1)
            pe.wait_ge(s_experts, 1)
            pe.wait_ge(s_wexp, 16 * (E // 4) * (1 + FC))
            run_quads(pe, step3, -1, 1, 9, QUADS)


_INS = ["x", "wq", "wk", "wv", "wo", "bq", "bk", "bv", "bo", "w_router_t", "gate_up", "down",
        "w_gate_t", "w_up_t", "w_down_t"]


def kernel(**inputs):
    import numpy as np
    import concourse.bacc as bacc
    from concourse.bass_utils import run_bass_kernel_spmd

    given = {n: np.asarray(a) for n, a in inputs.items()}
    laid = {
        "x": given["L0_attn_x"],
        "wq": given["L0_attn_Wq"], "wk": given["L0_attn_Wk"], "wv": given["L0_attn_Wv"], "wo": given["L0_attn_Wo"],
        "bq": given["L0_attn_bq"], "bk": given["L0_attn_bk"], "bv": given["L0_attn_bv"], "bo": given["L0_attn_bo"],
        "w_router_t": given["L0_ffn_w_router"].T, "gate_up": given["L0_ffn_gate_up_proj"],
        "down": given["L0_ffn_down_proj"], "w_gate_t": given["L0_ffn_w_gate"].T,
        "w_up_t": given["L0_ffn_w_up"].T, "w_down_t": given["L0_ffn_w_down"].T,
    }
    nc = bacc.Bacc("TRN2", target_bir_lowering=False, num_devices=1)
    arrays, args = {}, []
    for name in _INS:
        a = np.ascontiguousarray(laid[name])
        arrays[f"in_{name}"] = a
        args.append(nc.dram_tensor(f"in_{name}", a.shape, mybir.dt.from_np(a.dtype), kind="ExternalInput").ap())
    out = nc.dram_tensor("out_0", laid["x"].shape, F32, kind="ExternalOutput").ap()
    build(nc, *args, out)
    r = run_bass_kernel_spmd(nc, [arrays], core_ids=[0])
    return r.results[0]["out_0"]
```
